# Optimizing a Trainium2 kernel written in Bass

```python
import numpy as np
import jax
import jax.numpy as jnp

def _softmax(x, axis=-1):
    return jax.nn.softmax(x, axis=axis)

def _gelu(x):
    return jax.nn.gelu(x, approximate=True)

def _silu(x):
    return jax.nn.silu(x)

def _sigmoid(x):
    return jax.nn.sigmoid(x)

def _layernorm(x, axis=-1, eps=1e-05):
    m = jnp.mean(x, axis=axis, keepdims=True)
    v = jnp.var(x, axis=axis, keepdims=True)
    return (x - m) / jnp.sqrt(v + eps)

def _scatter_add(tgt, idx, src, axis=0):
    return tgt.at[idx].add(src)

def _segment_sum(src, seg, n):
    return jax.ops.segment_sum(src, seg, n)
kernel_name = 'mk_adj_ffn_d1_adj_r2_d6138a'

def setup_inputs(seed: int=0):
    np.random.seed(seed)
    _w = jnp.asarray

    def _rec_inputs():
        import jax
        import jax.numpy as jnp
        _gk = jax.random.key(seed)
        x = -0.0005207 + 1.001 * jax.random.normal(jax.random.fold_in(_gk, 1), (4096, 128), jnp.float32)
        _w = (1.0 + jnp.arange(4096, dtype=jnp.float32)) ** (-0.5)
        _w = _w / _w.mean()
        _pij = jnp.clip(0.000976562 * _w[:, None] * _w[None, :], 0.0, 1.0)
        _a = jax.random.uniform(jax.random.fold_in(_gk, 2), (4096, 4096)) < _pij
        _a = jnp.logical_or(_a, jnp.swapaxes(_a, -1, -2))
        _a = jnp.logical_or(_a, jnp.eye(4096, dtype=bool))
        _af = _a.astype(jnp.float32)
        _af = _af * jax.random.uniform(jax.random.fold_in(_gk, 3), (4096, 4096), jnp.float32, 0.05, 2.05)
        adj = _af
        return (x, adj)
    x, adj = _rec_inputs()

    def _L0_gnn_setup():
        import jax, jax.numpy as jnp
        import numpy as np
        N = 4096
        D = 128
        CUTOFF = 1.0
        MU = 1.0
        SIGMA = 0.5

        def sensitivity(r, mu, sigma):
            return jnp.exp(-(1.0 / r - 1.0 / mu) ** 2 / (2.0 * sigma * sigma))
        key = jax.random.key(seed)
        k_z, k_d, k_w = jax.random.split(key, 3)
        z = jax.random.normal(k_z, (N, D), dtype=jnp.float32)
        dist_matrix = jax.random.uniform(k_d, (N, N), dtype=jnp.float32) * 2.0 + 0.05
        W = jax.random.normal(k_w, (D, D), dtype=jnp.float32)
        B = jnp.zeros((D,), dtype=jnp.float32)
        return {'z': z, 'dist_matrix': dist_matrix, 'W': W, 'B': B}
    _L0_gnn_all = _L0_gnn_setup()
    _L0_gnn_in = {k: v for k, v in _L0_gnn_all.items() if k in ('W', 'B')}
    del _L0_gnn_all

    def _L0_ffn_setup():
        import jax, jax.numpy as jnp
        import numpy as np
        N_EXPERTS = 8
        TOP_K = 2
        key = jax.random.key(seed)
        ks = jax.random.split(key, 5)
        B, T, C, E, H = (8, 1024, 128, 8, 341)
        scale = 1.0 / np.sqrt(C)
        return {'x': jax.random.normal(ks[0], (B, T, C), dtype=jnp.float32), 'router_w': jax.random.normal(ks[1], (E, C), dtype=jnp.float32) * scale, 'w1': jax.random.normal(ks[2], (E, H, C), dtype=jnp.float32) * scale, 'w2': jax.random.normal(ks[3], (E, C, H), dtype=jnp.float32) * (1.0 / np.sqrt(H)), 'w3': jax.random.normal(ks[4], (E, H, C), dtype=jnp.float32) * scale}
    _L0_ffn_all = _L0_ffn_setup()
    _L0_ffn_in = {k: v for k, v in _L0_ffn_all.items() if k in ('router_w', 'w1', 'w2', 'w3')}
    del _L0_ffn_all
    return {'x': x, 'adj': adj, 'L0_gnn_W': _L0_gnn_in['W'], 'L0_gnn_B': _L0_gnn_in['B'], 'L0_ffn_router_w': _L0_ffn_in['router_w'], 'L0_ffn_w1': _L0_ffn_in['w1'], 'L0_ffn_w2': _L0_ffn_in['w2'], 'L0_ffn_w3': _L0_ffn_in['w3']}

def reference(x, adj, L0_gnn_W, L0_gnn_B, L0_ffn_router_w, L0_ffn_w1, L0_ffn_w2, L0_ffn_w3):
    import jax
    import jax.numpy as jnp

    def _L0_gnn_ref(z, dist_matrix, W, B):
        import jax, jax.numpy as jnp
        import numpy as np
        N = 4096
        D = 128
        CUTOFF = 1.0
        MU = 1.0
        SIGMA = 0.5

        def sensitivity(r, mu, sigma):
            return jnp.exp(-(1.0 / r - 1.0 / mu) ** 2 / (2.0 * sigma * sigma))
        msg = z @ W + B
        sens = sensitivity(dist_matrix, MU, SIGMA)
        weights = jnp.where(dist_matrix < CUTOFF, sens, 0.0)
        return weights @ msg

    def _L0_ffn_ref(x, router_w, w1, w2, w3):
        import jax, jax.numpy as jnp
        import numpy as np
        N_EXPERTS = 8
        TOP_K = 2
        B, T, C = x.shape
        flat = x.reshape(-1, C)
        logits = flat @ router_w.T
        probs = jax.nn.softmax(logits, axis=-1)
        topk_probs, topk_idx = jax.lax.top_k(probs, TOP_K)
        topk_probs = topk_probs / (jnp.sum(topk_probs, axis=-1, keepdims=True) + 1e-09)
        onehot = jax.nn.one_hot(topk_idx, N_EXPERTS, dtype=flat.dtype)
        gates = jnp.einsum('nk,nke->ne', topk_probs, onehot)
        h1 = jnp.einsum('nc,ehc->neh', flat, w1)
        h3 = jnp.einsum('nc,ehc->neh', flat, w3)
        h = jax.nn.silu(h1) * h3
        y = jnp.einsum('neh,ech->nec', h, w2)
        out = jnp.einsum('ne,nec->nc', gates, y)
        return out.reshape(B, T, C)
    x = x + _L0_gnn_ref(_layernorm(x, axis=-1), adj, L0_gnn_W, L0_gnn_B)
    x = x + _L0_ffn_ref(_layernorm(x, axis=-1)[None], L0_ffn_router_w, L0_ffn_w1, L0_ffn_w2, L0_ffn_w3)[0]
    return x

_drawn_inputs = setup_inputs


def setup_inputs(seed=0):
    import zlib

    import numpy as np

    out = dict(_drawn_inputs(seed))
    spreads = {'L0_gnn_B': (0.0, 0.418)}
    factors = {}
    for name, (base, spread) in spreads.items():
        noise = np.random.default_rng([zlib.crc32(name.encode()), seed]).standard_normal(out[name].shape)
        drawn = base * np.exp(spread * noise) if base else spread * noise
        out[name] = jnp.asarray(drawn.astype(out[name].dtype))
    for name, factor in factors.items():
        out[name] = (out[name] * factor).astype(out[name].dtype)
    return out
```

```python
import concourse.bass as bass
from concourse import mybir
from contextlib import ExitStack

F32 = mybir.dt.float32
U32 = mybir.dt.uint32
I32 = mybir.dt.int32
ALU = mybir.AluOpType
ACT = mybir.ActivationFunctionType
AX_X = mybir.AxisListType.X
P = 128
LN_EPS = 1e-5
TINY = 2.0 ** -60


def gnn_moe_layer(nc, x, adj, gnn_w, gnn_b, router_w, w1, w2, w3, out):
    N, D = x.shape
    K = N // P
    TG = 4
    G = K // TG
    SRC = 8
    C = K // SRC
    PARTS = 4
    SP = SRC // PARTS
    GW = TG * P
    HALF = SRC // 2
    U = G * C
    E, H, _ = w1.shape
    HT = -(-H // P)
    HL = H - (HT - 1) * P
    FT = E * H // P
    FL = E * H - FT * P
    CAP = N + P
    TILES = 2 * N // P + E
    ROW = D + 2
    GB, IDB = D, D + 1
    RING = 8
    PER = 16 // RING
    assert TILES % RING == 0

    slots = nc.dram_tensor("slots", [E * CAP + E * P, ROW], F32, kind="Internal").ap()
    results = nc.dram_tensor("results", [2 * N + 2 * E * P, D], F32, kind="Internal").ap()

    adj_v = adj.rearrange("(g b p) (c j) -> g c p b j", b=TG, p=P, c=C)
    x_v = x.rearrange("(k p) d -> p k d", p=P)
    out_v = out.rearrange("(k p) d -> p k d", p=P)

    weight_groups = []
    with ExitStack() as ctx:
        def sb(name, shape, dt=F32):
            return ctx.enter_context(nc.sbuf_tensor(name, shape, dt))

        def pb(name, shape, dt=F32):
            return ctx.enter_context(nc.psum_tensor(name, shape, dt))

        def sem(name):
            return ctx.enter_context(nc.semaphore(name))

        r = sb("r", [P, C, TG, SRC * P])
        y = sb("y", [P, 2, SRC, GW])
        w = sb("w", [P, 2, SRC, GW])
        xs = sb("xs", [P, K, D])
        msg = sb("msg", [P, K, D])
        tmp = sb("tmp", [P, 2, K, D])
        xn, xnT = tmp[:, 0], tmp[:, 1]
        ident = sb("ident", [P, P])
        wg = sb("wg", [P, D])
        bg = sb("bg", [P, D])
        stat = sb("stat", [P, 6, K])
        epsT = sb("epsT", [P, 2])
        bm2 = sb("bm2", [P, 1])
        upper = sb("upper", [P, P])
        ones = sb("ones", [P, P])
        rev = sb("rev", [P, E])
        ids = sb("ids", [P, K, 2], U32)
        pid = sb("pid", [P, E], I32)
        rows = sb("rows", [P, 2, TG, ROW])
        pad = sb("pad", [P, E, ROW])
        pad_at = sb("pad_at", [P, E], U32)
        rw = sb("rw", [E, D])
        rwT = sb("rwT", [P, E])
        bnst = sb("bnst", [P, TG, 6])
        mv = sb("mv", [P, TG, 2])
        st2 = sb("st2", [P, 4, TG])
        lg = sb("lg", [P, 8, TG, E])
        sm = sb("sm", [P, 10, TG])
        soft = sb("soft", [P, TG * E + TG])
        softe = sb("softe", [P, TG * E + TG])
        base = sb("base", [P, E])
        slot_at = sb("slot_at", [P, TG, 2], U32)
        tau = sb("tau", [1, TILES])
        nt = sb("nt", [1, 6, E])
        nti = sb("nti", [1, 2, E], I32)
        tabi = sb("tabi", [1, 2, TILES + 2 * RING], I32)

        left = tmp[:, 0].rearrange("p k d -> p (k d)")[:, K * D - 2 * GW:]
        aggT, xn2T = left[:, 0:GW], left[:, GW:]
        left = tmp[0:1, 1].rearrange("p k d -> p (k d)")[:, K * D - 2 * GW:]
        tab = left[:, 0:TILES * E].rearrange("p (t e) -> p t e", e=E)
        tabf = left[:, TILES * E:TILES * (E + 3)].rearrange("p (a t) -> p a t", a=3)
        def flat(v, w_):
            return v.rearrange("p a b -> p (a b)")[:, 0:w_]
        w1raw = flat(r[:, 0], (FT + 1) * D).rearrange("p (t d) -> p t d", d=D)
        w3raw = flat(r[:, 1], (FT + 1) * D).rearrange("p (t d) -> p t d", d=D)
        w2raw = flat(r[:, 2], E * H).rearrange("p (e h) -> p e h", h=H)
        w2T = flat(r[:, 3], E * HT * D)
        w1T = tmp[:, 0].rearrange("p k d -> p (k d)")[:, 0:E * H]
        w3T = tmp[:, 1].rearrange("p k d -> p (k d)")[:, 0:E * H]
        yf = y[:].rearrange("p a s n -> p (a s n)")
        xt = yf[:, 0:RING * ROW].rearrange("p (i n) -> p i n", n=ROW)
        at = RING * ROW
        xtT = yf[:, at:at + 2 * P].rearrange("p (i n) -> p i n", n=P)
        at += 2 * P
        sil = yf[:, at:at + 2 * HT * P].rearrange("p (i n) -> p i n", n=HT * P)
        at += 2 * HT * P
        hid = yf[:, at:at + 2 * HT * P].rearrange("p (i n) -> p i n", n=HT * P)
        at += 2 * HT * P
        hidT = yf[:, at:at + 2 * HT * P].rearrange("p (i j n) -> p i j n", j=HT, n=P)
        at += 2 * HT * P
        yo = yf[:, at:at + RING * D].rearrange("p (i n) -> p i n", n=D)
        res = w[:].rearrange("p a s n -> p (a s n)").rearrange("p (k c d) -> p k c d", c=2, d=D)

        pT = pb("pT", [P, 2, SP, GW])
        pAgg = pb("pAgg", [P, GW])
        pX = pb("pX", [P, TG, P])
        pM = pb("pM", [P, 2, TG, D])
        pXn = pM[:, 0]
        pSm = pM[:, 1].rearrange("p b d -> p (b d)")
        pLogits = pSm[:, 0:TG * E].rearrange("p (b e) -> p b e", e=E)
        pRank = pSm[:, 128:128 + TG * E].rearrange("p (b e) -> p b e", e=E)
        pTot = pSm[:, 256:256 + E]
        pH = [pT[:, 0].rearrange("p s n -> p (s n)"), pT[:, 1].rearrange("p s n -> p (s n)")]
        pHT = pM[:, 0, 0:HT]
        pXT = pX[:, 0]
        pY = pM[:, 1, 0]
        pW = [pT[:, 0, 0], pT[:, 0, 1], pT[:, 1, 0], pT[:, 1, 1]]

        r_loaded = [sem(f"r_loaded{c}") for c in range(C)]
        x_loaded, wg_loaded, bg_loaded = sem("x_loaded"), sem("wg_loaded"), sem("bg_loaded")
        id0, ident_ready, consts_ready = sem("id0"), sem("ident_ready"), sem("consts_ready")
        masked = sem("masked")
        part_T = sem("part_T")
        ln_done, e1_done, q_done, e2_done = sem("ln_done"), sem("e1_done"), sem("q_done"), sem("e2_done")
        agg_done = sem("agg_done")
        aggT_copied, x2_T, x2_done = sem("aggT_copied"), sem("x2_T"), sem("x2_done")
        dve_step, act_step = sem("dve_step"), sem("act_step")
        xn_T, xnT_copied, msg_mm, msg_ready = sem("xn_T"), sem("xnT_copied"), sem("msg_mm"), sem("msg_ready")
        out_stored = sem("out_stored")
        rw_loaded, w_loaded = sem("rw_loaded"), [sem(f"w_loaded{n}") for n in range(5)]
        tables_ready, pad_zeroed, pad_ids = sem("tables_ready"), sem("pad_zeroed"), sem("pad_ids")
        rw_T, rwT_copied = sem("rw_T"), sem("rwT_copied")
        route, ln2_act = sem("route"), sem("ln2_act")
        var2_ready, rows_ready, xn2_T, xn2T_copied = sem("var2_ready"), sem("rows_ready"), sem("xn2_T"), sem("xn2T_copied")
        logits_mm, soft_in, soft_done, picked, rank_mm = (sem("logits_mm"), sem("soft_in"), sem("soft_done"),
                                                         sem("picked"), sem("rank_mm"))
        slots_ready = sem("slots_ready")
        scattered = [sem(f"scattered{n}") for n in range(2 * TG)]
        padded = [sem(f"padded{n}") for n in range(E)]
        dummies_stored = sem("dummies_stored")
        plan, plan_ready = sem("plan"), sem("plan_ready")
        w_T, w_copied = sem("w_T"), sem("w_copied")
        xt_loaded = [sem(f"xt_loaded{i}") for i in range(RING)]
        yt_stored = [sem(f"yt_stored{i}") for i in range(RING)]
        xt_T, xtT_copied, h_mm, sil_done, hid_ready, hid_T, hidT_copied, y_mm, y_out = (
            sem("xt_T"), sem("xtT_copied"), sem("h_mm"), sem("sil_done"), sem("hid_ready"), sem("hid_T"),
            sem("hidT_copied"), sem("y_mm"), sem("y_out"))
        res_loaded = [sem(f"res_loaded{n}") for n in range(4)]
        res_added = sem("res_added")
        stood = sem("stood")
        NC = 4
        KC = K // NC

        def tile_steps(step):
            return step

        weight_groups += [(dst, P, lo, min(lo + 4 * P, E * H)) for dst in (w1T, w3T) for lo in range(0, E * H, 4 * P)]
        weight_groups += [(w2T, P, HT * D * e, HT * D * e + (HT - 1) * D) for e in range(E)]
        weight_groups += [(w2T, HL, HT * D * e + (HT - 1) * D, HT * D * (e + 1)) for e in range(E)]

        block = ctx.enter_context(nc.Block())

        w1f, w3f = w1.rearrange("e h d -> (e h) d"), w3.rearrange("e h d -> (e h) d")

        def load_at(sp, t, i):
            at = sp.value_load(tabi[0:1, 0, bass.ds(t, 1)], min_val=0, max_val=E * CAP + (E - 1) * P)
            sp.dma_start(xt[:, i], slots[bass.ds(at, P), :]).then_inc(xt_loaded[i], 16)

        @block.sync
        def _(sp):
            def load(g, c):
                sp.dma_start(r[:, c], adj_v[g, c]).then_inc(r_loaded[c], 16)

            sp.dma_start(xs[:], x_v).then_inc(x_loaded, 16)
            for c in range(C):
                load(0, c)
            sp.dma_start(rw[:], router_w).then_inc(rw_loaded, 16)
            sp.dma_start(wg[:], gnn_w).then_inc(wg_loaded, 16)
            sp.dma_start(bg[:], gnn_b.rearrange("(a d) -> a d", a=1).to_broadcast([P, D])).then_inc(bg_loaded, 16)
            with sp.Fori(1, G) as g:
                for c in range(C):
                    sp.wait_ge(part_T, PARTS * (C * g + c - C + 1))
                    load(g, c)
            for n, (dst, src) in enumerate((
                    (w1raw[:, 0:FT], w1f[0:FT * P].rearrange("(t p) d -> p t d", p=P)),
                    (w1raw[0:FL, FT], w1f[FT * P:E * H]),
                    (w3raw[:, 0:FT], w3f[0:FT * P].rearrange("(t p) d -> p t d", p=P)),
                    (w3raw[0:FL, FT], w3f[FT * P:E * H]),
                    (w2raw, w2.rearrange("e d h -> d e h")))):
                if n % 2 == 0:
                    sp.wait_ge(part_T, PARTS * (U - C + n // 2 + 1))
                sp.dma_start(dst, src).then_inc(w_loaded[n], 16)

            sp.wait_ge(plan_ready, 1)
            sp.wait_ge(dummies_stored, 16)
            for e in range(E):
                sp.wait_ge(padded[e], 16)
            for n in range(2 * TG):
                sp.wait_ge(scattered[n], 16 * G)
            for i in range(RING):
                load_at(sp, i, i)
            with sp.Fori(RING, TILES, RING) as t:
                for i in range(RING):
                    sp.wait_ge(yt_stored[i], PER * t)
                    sp.sem_inc(stood, 1)
                    load_at(sp, t + i, i)
            for i in range(RING):
                sp.wait_ge(yt_stored[i], 16 * (TILES // RING))
            rv = results[0:2 * N].rearrange("(k p c) d -> p k c d", p=P, c=2)
            for n in range(NC):
                sp.dma_start(res[:, KC * n:KC * n + KC], rv[:, KC * n:KC * n + KC]).then_inc(res_loaded[n], 16)
            for n in range(NC):
                sp.wait_ge(res_added, 2 * n + 2)
                sp.dma_start(out_v[:, KC * n:KC * n + KC], xs[:, KC * n:KC * n + KC]).then_inc(out_stored, 16)
            sp.wait_ge(out_stored, 16 * NC)

        @block.gpsimd
        def _(pool):
            nc.gpsimd.memset(ident[:], 0.0).then_inc(id0, 1)
            pool.wait_ge(id0, 1)
            nc.gpsimd.affine_select(out=ident[:], in_=ident[:], compare_op=ALU.not_equal, fill=1.0, base=0,
                                    pattern=[[-1, P]], channel_multiplier=1).then_inc(ident_ready, 1)
            nc.gpsimd.memset(epsT[:, 0:1], TINY)
            nc.gpsimd.memset(bm2[:], -2.0)
            nc.gpsimd.memset(epsT[:, 1:2], LN_EPS).then_inc(consts_ready, 1)
            nc.gpsimd.memset(ones[:], 1.0).then_inc(id0, 1)
            pool.wait_ge(id0, 2)
            nc.gpsimd.affine_select(out=upper[:], in_=ones[:], compare_op=ALU.is_gt, fill=0.0, base=0,
                                    pattern=[[1, P]], channel_multiplier=-1)
            nc.gpsimd.iota(ids[:], [[2 * P, K], [1, 2]], base=0, channel_multiplier=2)
            nc.gpsimd.iota(pid[:], [[0, E]], base=0, channel_multiplier=1)
            nc.gpsimd.iota(rev[:], [[-1, E]], base=E, channel_multiplier=0, allow_small_or_imprecise_dtypes=True)
            nc.gpsimd.iota(base[:], [[CAP, E]], base=0, channel_multiplier=0, allow_small_or_imprecise_dtypes=True)
            nc.gpsimd.iota(tau[:], [[1, TILES]], base=0, channel_multiplier=0,
                           allow_small_or_imprecise_dtypes=True).then_inc(tables_ready, 1)
            nc.gpsimd.memset(pad[:], 0.0).then_inc(pad_zeroed, 1)
            pool.wait_ge(pad_zeroed, 1)
            nc.gpsimd.iota(pad[:, :, IDB:IDB + 1].bitcast(U32), [[P, E], [0, 1]], base=2 * N + E * P,
                           channel_multiplier=1).then_inc(pad_ids, 1)
            pool.wait_ge(pad_ids, 1)
            pool.dma_start(slots[E * CAP:E * CAP + E * P].rearrange("(e p) n -> p e n", p=P),
                           pad[:]).then_inc(dummies_stored, 16)
            pool.wait_ge(dummies_stored, 16)
            nc.gpsimd.iota(pad[:, :, IDB:IDB + 1].bitcast(U32), [[P, E], [0, 1]], base=2 * N,
                           channel_multiplier=1).then_inc(pad_ids, 1)

            def scatter_group(g):
                pool.wait_ge(slots_ready, g + 1)
                pool.sem_inc(stood, 1)
                for ch in range(2):
                    for b in range(TG):
                        pool.indirect_dma_start(slots, bass.IndirectOffsetOnAxis(slot_at[:, b, ch:ch + 1], 0),
                                                rows[:, ch, b], None).then_inc(scattered[TG * ch + b], 16)
            with pool.Fori(0, G) as g:
                scatter_group(g)
            pool.wait_ge(plan_ready, 1)
            pool.wait_ge(pad_ids, 2)
            for e in range(E):
                pool.indirect_dma_start(slots, bass.IndirectOffsetOnAxis(pad_at[:, e:e + 1], 0), pad[:, e],
                                        None).then_inc(padded[e], 16)
            with pool.Fori(0, TILES, RING) as t:
                for i in range(RING):
                    pool.wait_ge(y_out, t + i + 1)
                    pool.sem_inc(stood, 1)
                    pool.indirect_dma_start(results, bass.IndirectOffsetOnAxis(xt[:, i, IDB:IDB + 1].bitcast(U32), 0),
                                            yo[:, i], None).then_inc(yt_stored[i], 16)

        @block.scalar
        def _(act):
            def ln_part(u, c, h):
                act.wait_ge(part_T, PARTS * u + h + 1)
                nc.scalar.activation(y[:, c % 2, SP * h:SP * (h + 1)], pT[:, h % 2], ACT.Ln,
                                     bias=epsT[:, 0:1]).then_inc(ln_done, 1)

            def unit(u, c, ahead, mid=None):
                act.wait_ge(ln_done, PARTS * u + PARTS)
                for h in range(2):
                    v = y[:, c % 2, HALF * h:HALF * (h + 1)]
                    nc.scalar.activation(v, v, ACT.Exp, scale=-1.0).then_inc(e1_done, 1)
                if ahead:
                    if not (isinstance(u, int) and u == 0):
                        act.wait_ge(e2_done, 2 * u)
                    for h in range(PARTS):
                        ln_part(u + 1, c + 1, h)
                if mid:
                    mid()
                for h in range(2):
                    act.wait_ge(q_done, 2 * u + h + 1)
                    if h == 0 and not (isinstance(u, int) and u < 2):
                        act.wait_ge(agg_done, u - 1)
                    nc.scalar.activation(w[:, c % 2, HALF * h:HALF * (h + 1)], y[:, c % 2, HALF * h:HALF * (h + 1)],
                                         ACT.Exp, scale=-2.0, bias=bm2[:, 0:1]).then_inc(e2_done, 1)

            def rstd2(g):
                act.wait_ge(var2_ready, g + 1)
                nc.scalar.activation(st2[:, 0], mv[:, :, 1], ACT.Ln, bias=epsT[:, 1:2]).then_inc(ln2_act, 1)
                act.wait_ge(ln2_act, 2 * g + 1)
                nc.scalar.activation(st2[:, 1], st2[:, 0], ACT.Exp, scale=-0.5).then_inc(ln2_act, 1)

            def softmax_exp(g):
                act.wait_ge(soft_in, g + 1)
                nc.scalar.activation(softe[:], soft[:], ACT.Exp).then_inc(soft_done, 1)

            act.wait_ge(consts_ready, 1)
            nc.scalar.preload_act_table_set("natural_log_exp_and_others")
            for h in range(PARTS):
                ln_part(0, 0, h)
            act.wait_ge(dve_step, 2)
            nc.scalar.activation(xnT, xn, ACT.Square).then_inc(act_step, 1)
            act.wait_ge(dve_step, 3)
            nc.scalar.activation(stat[:, 2], stat[:, 1], ACT.Ln, scale=1.0 / D, bias=epsT[:, 1:2]).then_inc(act_step, 1)
            act.wait_ge(act_step, 2)
            nc.scalar.activation(stat[:, 3], stat[:, 2], ACT.Exp, scale=-0.5).then_inc(act_step, 1)
            def group(g, first=False, last=False):
                for c in range(C):
                    unit(C * g + c, c, not last or c < C - 1,
                         mid=(lambda: softmax_exp(g - 1)) if c == 2 and not first else None)
                    if c == 0 and not first:
                        rstd2(g - 1)
            group(0, first=True)
            group(1)
            with act.Fori(2, G - 1) as g:
                group(g)
            group(G - 1, last=True)
            rstd2(G - 1)
            softmax_exp(G - 1)

            def silu(t, i):
                act.wait_ge(h_mm, t + 1)
                if not (isinstance(t, int) and t < 2):
                    act.wait_ge(hid_ready, t - 1)
                nc.scalar.activation(sil[:, i % 2, 0:H], pH[i % 2][:, 0:H], ACT.Silu).then_inc(sil_done, 1)

            def copy_hidT(t, i):
                act.wait_ge(hid_T, t + 1)
                if not (isinstance(t, int) and t < 2):
                    act.wait_ge(y_mm, t - 1)
                nc.scalar.activation(hidT[:, i % 2, 0:HT - 1], pHT[:, 0:HT - 1], ACT.Copy)
                nc.scalar.activation(hidT[0:HL, i % 2, HT - 1], pHT[0:HL, HT - 1], ACT.Copy).then_inc(hidT_copied, 1)

            def tile_act(t, i):
                if not isinstance(t, int) or t + 1 < TILES:
                    silu(t + 1, i + 1)
                copy_hidT(t, i)

            silu(0, 0)
            for t in range(RING):
                tile_act(t, t)
            with act.Fori(RING, TILES - RING, RING) as t:
                for i in range(RING):
                    tile_act(t + i, i)
            for t in range(TILES - RING, TILES):
                tile_act(t, t)

        @block.vector
        def _(dve):
            def mask(g, c):
                dve.wait_ge(r_loaded[c], 16 * (g + 1))
                v = r[:, c]
                nc.vector.scalar_tensor_tensor(out=v, in0=v, scalar=1.0, in1=v, op0=ALU.is_lt,
                                               op1=ALU.mult).then_inc(masked, 1)

            def exponent(u, c, mid=None):
                for h in range(2):
                    if h and mid:
                        mid()
                    dve.wait_ge(e1_done, 2 * u + h + 1)
                    v = y[:, c % 2, HALF * h:HALF * (h + 1)]
                    nc.vector.scalar_tensor_tensor(out=v, in0=v, scalar=2.0, in1=v, op0=ALU.subtract,
                                                   op1=ALU.mult).then_inc(q_done, 1)

            def copy_aggT(g):
                dve.wait_ge(agg_done, C * (g + 1))
                if not isinstance(g, int) or g > 0:
                    dve.wait_ge(x2_T, g)
                nc.vector.tensor_copy(aggT[:], pAgg[:]).then_inc(aggT_copied, 1)

            def add_x(g):
                dve.wait_ge(x2_T, g + 1)
                v = xs[:, bass.ds(TG * g, TG), :] if not isinstance(g, int) else xs[:, TG * g:TG * g + TG, :]
                nc.vector.tensor_tensor(v, pX[:], v, ALU.add).then_inc(x2_done, 1)

            mask(0, 0)
            mask(0, 1)
            dve.wait_ge(x_loaded, 16)
            nc.vector.reduce_sum(stat[:, 0], xs[:], AX_X).then_inc(dve_step, 1)
            dve.wait_ge(dve_step, 1)
            nc.vector.scalar_tensor_tensor(out=xn, in0=stat[:, 0].unsqueeze(2).to_broadcast([P, K, D]), scalar=-1.0 / D,
                                           in1=xs[:], op0=ALU.mult, op1=ALU.add).then_inc(dve_step, 1)
            dve.wait_ge(act_step, 1)
            nc.vector.reduce_sum(stat[:, 1], xnT, AX_X).then_inc(dve_step, 1)
            dve.wait_ge(act_step, 3)
            nc.vector.tensor_scalar(stat[:, 4], stat[:, 1], -0.5 / D, -0.5 * LN_EPS, ALU.mult, ALU.add).then_inc(dve_step, 1)
            nc.vector.tensor_tensor(stat[:, 5], stat[:, 3], stat[:, 3], ALU.mult).then_inc(dve_step, 1)
            dve.wait_ge(dve_step, 5)
            nc.vector.tensor_tensor(stat[:, 5], stat[:, 5], stat[:, 4], ALU.mult).then_inc(dve_step, 1)
            dve.wait_ge(dve_step, 6)
            nc.vector.scalar_tensor_tensor(out=stat[:, 4], in0=stat[:, 5], scalar=1.5, in1=stat[:, 3], op0=ALU.add,
                                           op1=ALU.mult).then_inc(dve_step, 1)
            dve.wait_ge(dve_step, 7)
            nc.vector.tensor_tensor(xn, xn, stat[:, 4].unsqueeze(2).to_broadcast([P, K, D]), ALU.mult).then_inc(dve_step, 1)
            for n in range(K // TG):
                dve.wait_ge(xn_T, n + 1)
                nc.vector.tensor_copy(xnT[:, TG * n:TG * n + TG], pM[:, n % 2]).then_inc(xnT_copied, 1)
            dve.wait_ge(bg_loaded, 16)
            for n in range(K // TG):
                dve.wait_ge(msg_mm, n + 1)
                nc.vector.tensor_tensor(msg[:, TG * n:TG * n + TG], pM[:, n % 2],
                                        bg[:].unsqueeze(1).to_broadcast([P, TG, D]), ALU.add).then_inc(msg_ready, 1)

            STEPS = 37

            class Chain:
                def __init__(self, g, n):
                    self.g, self.n = g, n

                def __call__(self, ins):
                    ins.then_inc(route, 1)
                    self.n += 1
                    dve.wait_ge(route, STEPS * self.g + self.n)

            def moments(g):
                k0 = TG * g
                dve.wait_ge(x2_done, g + 1)
                dve.sem_inc(stood, 1)
                for b in range(TG):
                    nc.vector.bn_stats(bnst[:, b], xs[:, bass.ds(k0 + b, 1)].rearrange("p a d -> p (a d)")).then_inc(route, 1)
                dve.wait_ge(route, STEPS * g + TG)
                dve.sem_inc(stood, 1)
                for b in range(TG):
                    last = nc.vector.bn_aggr(mv[:, b], bnst[:, b])
                last.then_inc(var2_ready, 1)

            def normalise(g):
                dve.wait_ge(ln2_act, 2 * g + 2)
                if not isinstance(g, int) or g > 0:
                    for n in range(2 * TG):
                        dve.wait_ge(scattered[n], 16 * g)
                ch = Chain(g, TG)
                ch(nc.vector.tensor_scalar(st2[:, 2], mv[:, :, 1], -0.5, -0.5 * LN_EPS, ALU.mult, ALU.add))
                ch(nc.vector.tensor_tensor(st2[:, 3], st2[:, 1], st2[:, 1], ALU.mult))
                ch(nc.vector.tensor_tensor(st2[:, 3], st2[:, 3], st2[:, 2], ALU.mult))
                ch(nc.vector.scalar_tensor_tensor(out=st2[:, 2], in0=st2[:, 3], scalar=1.5, in1=st2[:, 1], op0=ALU.add,
                                                  op1=ALU.mult))
                for c_ in range(2):
                    for b in range(TG):
                        last = nc.vector.tensor_scalar(rows[:, c_, b, 0:D],
                                                       xs[:, bass.ds(TG * g + b, 1)].rearrange("p a d -> p (a d)"),
                                                       mv[:, b, 0:1], st2[:, 2, b:b + 1], ALU.subtract, ALU.mult)
                last.then_inc(rows_ready, 1)

            def copy_xn2T(g):
                dve.wait_ge(xn2_T, g + 1)
                if not isinstance(g, int) or g > 0:
                    dve.wait_ge(logits_mm, g)
                nc.vector.tensor_copy(xn2T[:], pXn.rearrange("p b d -> p (b d)")).then_inc(xn2T_copied, 1)

            def bc(v):
                return v.unsqueeze(2).to_broadcast([P, TG, E])

            revb = rev[:].unsqueeze(1).to_broadcast([P, TG, E])

            def pick(g):
                dve.wait_ge(logits_mm, g + 1)
                ch = Chain(g, TG + 4)
                L, A, B, t0, M = lg[:, 0], lg[:, 1], lg[:, 2], lg[:, 3], lg[:, 4]
                ch(nc.vector.tensor_copy(L, pLogits))
                for n, (src, one_hot) in enumerate(((L, A), (lg[:, 5], B))):
                    if n:
                        ch(nc.vector.scalar_tensor_tensor(out=src, in0=A, scalar=-3.0e38, in1=L, op0=ALU.mult, op1=ALU.add))
                    ch(nc.vector.reduce_max(sm[:, n], src, AX_X))
                    ch(nc.vector.tensor_tensor(t0, src, bc(sm[:, n]), ALU.is_equal))
                    ch(nc.vector.tensor_tensor(t0, t0, revb, ALU.mult))
                    ch(nc.vector.reduce_max(sm[:, 2], t0, AX_X))
                    ch(nc.vector.tensor_tensor(one_hot, t0, bc(sm[:, 2]), ALU.is_equal))
                nc.vector.tensor_tensor(M, A, B, ALU.add).then_inc(picked, 1)
                nc.vector.tensor_tensor(soft[:, 0:TG * E].rearrange("p (b e) -> p b e", e=E), L, bc(sm[:, 0]), ALU.subtract)
                nc.vector.tensor_tensor(soft[:, TG * E:], sm[:, 1], sm[:, 0], ALU.subtract).then_inc(soft_in, 1)

            def place(g):
                ch = Chain(g, TG + 4 + 12)
                A, B, V, VA, VB = lg[:, 1], lg[:, 2], lg[:, 3], lg[:, 6], lg[:, 7]
                dve.wait_ge(rank_mm, g + 1)
                ch(nc.vector.tensor_tensor(V, pRank, base[:].unsqueeze(1).to_broadcast([P, TG, E]), ALU.add))
                ch(nc.vector.tensor_tensor(base[:], pTot, base[:], ALU.add))
                ch(nc.vector.tensor_tensor(VA, V, A, ALU.mult))
                ch(nc.vector.tensor_tensor(VB, V, B, ALU.mult))
                ch(nc.vector.reduce_sum(sm[:, 3], VA, AX_X))
                ch(nc.vector.reduce_sum(sm[:, 4], VB, AX_X))
                ch(nc.vector.tensor_copy(slot_at[:, :, 0], sm[:, 3]))
                ch(nc.vector.tensor_copy(slot_at[:, :, 1], sm[:, 4]))
                for c_ in range(2):
                    ch(nc.vector.tensor_copy(rows[:, c_, :, IDB:IDB + 1].bitcast(U32), ids[:, bass.ds(TG * g, TG), c_:c_ + 1]))
                dve.wait_ge(soft_done, g + 1)
                ch(nc.vector.reduce_sum(sm[:, 5], softe[:, 0:TG * E].rearrange("p (b e) -> p b e", e=E), AX_X))
                ch(nc.vector.reciprocal(sm[:, 6], sm[:, 5]))
                ch(nc.vector.tensor_tensor(sm[:, 7], softe[:, TG * E:], sm[:, 6], ALU.mult))
                ch(nc.vector.tensor_tensor(sm[:, 8], sm[:, 6], sm[:, 7], ALU.add))
                ch(nc.vector.tensor_scalar(sm[:, 8], sm[:, 8], 1e-9, None, ALU.add))
                ch(nc.vector.reciprocal(sm[:, 9], sm[:, 8]))
                ch(nc.vector.tensor_tensor(rows[:, 0, :, GB], sm[:, 6], sm[:, 9], ALU.mult))
                nc.vector.tensor_tensor(rows[:, 1, :, GB], sm[:, 7], sm[:, 9], ALU.mult).then_inc(slots_ready, 1)
                return ch.n

            def group(g, first=False, last=False):
                for c in range(C):
                    if not (last and c >= C - 2):
                        mask(g + (c + 2) // C, (c + 2) % C)
                    mid, end = (((lambda: copy_aggT(g - 1)), (lambda: (add_x(g - 1), moments(g - 1)))),
                                ((lambda: normalise(g - 1)), (lambda: copy_xn2T(g - 1))),
                                ((lambda: pick(g - 1)), (lambda: place(g - 1))),
                                (None, None))[c]
                    exponent(C * g + c, c, None if first else mid)
                    if end and not first:
                        end()
            dve.wait_ge(tables_ready, 1)
            dve.wait_ge(rw_T, 1)
            nc.vector.tensor_copy(rwT[:], pAgg[:, 0:E]).then_inc(rwT_copied, 1)
            group(0, first=True)
            group(1)
            with dve.Fori(2, G - 1) as g:
                group(g)
            group(G - 1, last=True)
            copy_aggT(G - 1)
            add_x(G - 1)
            moments(G - 1)
            normalise(G - 1)
            copy_xn2T(G - 1)
            pick(G - 1)
            assert place(G - 1) == STEPS + 0, "STEPS"

            n = [0]

            def link(ins):
                ins.then_inc(plan, 1)
                n[0] += 1
                dve.wait_ge(plan, n[0])
            b0 = base[0:1, :]
            link(nc.vector.tensor_tensor(sm[:, 0:2].rearrange("p a b -> p (a b)"), base[:], pid[:], ALU.add))
            link(nc.vector.tensor_copy(pad_at[:], sm[:, 0:2].rearrange("p a b -> p (a b)")))
            link(nc.vector.scalar_tensor_tensor(out=nt[:, 0], in0=rev[0:1, :], scalar=float(CAP), in1=b0, op0=ALU.mult,
                                                op1=ALU.add))
            link(nc.vector.tensor_scalar(nti[:, 0], nt[:, 0], float(P - 1 - E * CAP), None, ALU.add))
            link(nc.vector.tensor_scalar(nti[:, 1], nti[:, 0], P.bit_length() - 1, None, ALU.logical_shift_right))
            link(nc.vector.tensor_copy(nt[:, 1], nti[:, 1]))
            link(nc.vector.tensor_copy(nt[:, 2, 0:1], nt[:, 1, 0:1]))
            for e in range(1, E):
                link(nc.vector.tensor_tensor(nt[:, 2, e:e + 1], nt[:, 2, e - 1:e], nt[:, 1, e:e + 1], ALU.add))
            link(nc.vector.tensor_scalar(nt[:, 3], nt[:, 1], -float(P), float(CAP), ALU.mult, ALU.add))
            tb = tau[:].unsqueeze(2).to_broadcast([1, TILES, E])
            link(nc.vector.tensor_tensor(tab[:], tb, nt[:, 2:3].to_broadcast([1, TILES, E]), ALU.is_ge))
            link(nc.vector.reduce_sum(tabf[:, 0], tab[:], AX_X))
            link(nc.vector.tensor_scalar(tabi[:, 1, 0:TILES], tabf[:, 0], float(E - 1), None, ALU.min))
            link(nc.vector.tensor_tensor(tab[:], tab[:], nt[:, 3:4].to_broadcast([1, TILES, E]), ALU.mult))
            link(nc.vector.reduce_sum(tabf[:, 1], tab[:], AX_X))
            link(nc.vector.scalar_tensor_tensor(out=tabf[:, 2], in0=tau[:], scalar=float(P), in1=tabf[:, 1], op0=ALU.mult,
                                                op1=ALU.add))
            nc.vector.tensor_copy(tabi[:, 0, 0:TILES], tabf[:, 2]).then_inc(plan_ready, 1)

            for n_, (dst, rows_, lo, hi) in enumerate(weight_groups):
                dve.wait_ge(w_T, n_ + 1)
                nc.vector.tensor_copy(dst[0:rows_, lo:hi], pW[n_ % 4][0:rows_, 0:hi - lo]).then_inc(w_copied, 1)

            def copy_xt(t, i):
                dve.wait_ge(xt_T, t + 1)
                if not (isinstance(t, int) and t < 2):
                    dve.wait_ge(h_mm, t - 1)
                nc.vector.tensor_copy(xtT[:, i % 2], pXT).then_inc(xtT_copied, 1)

            def gated(t, i):
                dve.wait_ge(y_mm, t + 1)
                if not (isinstance(t, int) and t < RING):
                    dve.wait_ge(yt_stored[i % RING], 16 * (t // RING) if isinstance(t, int) else PER * (t - i % RING))
                nc.vector.tensor_scalar(yo[:, i % RING], pY, xt[:, i % RING, GB:GB + 1], None, ALU.mult).then_inc(y_out, 1)

            def hidden(t, i):
                dve.wait_ge(sil_done, t + 1)
                if not (isinstance(t, int) and t < 2):
                    dve.wait_ge(hid_T, t - 1)
                nc.vector.tensor_tensor(hid[:, i % 2, 0:H], pH[i % 2][:, 512:512 + H], sil[:, i % 2, 0:H],
                                        ALU.mult).then_inc(hid_ready, 1)

            def tile_dve(t, i):
                known = isinstance(t, int)
                if not known or t + 2 < TILES:
                    copy_xt(t + 2, i + 2)
                if not known or t > 0:
                    gated(t - 1, (i - 1) % RING)
                if not known or t + 1 < TILES:
                    hidden(t + 1, i + 1)

            copy_xt(0, 0)
            copy_xt(1, 1)
            hidden(0, 0)
            for t in range(RING):
                tile_dve(t, t)
            with dve.Fori(RING, TILES - RING, RING) as t:
                for i in range(RING):
                    tile_dve(t + i, i)
            for t in range(TILES - RING, TILES):
                tile_dve(t, t)
            gated(TILES - 1, RING - 1)
            for n_ in range(NC):
                dve.wait_ge(res_loaded[n_], 16)
                for c_ in range(2):
                    v = xs[:, KC * n_:KC * n_ + KC]
                    if c_:
                        dve.wait_ge(res_added, 2 * n_ + 1)
                    nc.vector.tensor_tensor(v, v, res[:, KC * n_:KC * n_ + KC, c_], ALU.add).then_inc(res_added, 1)

        @block.tensor
        def _(pe):
            def part(u, c, h):
                pe.wait_ge(masked, u + 1)
                if not (isinstance(u, int) and u == 0 and h < 2):
                    pe.wait_ge(ln_done, PARTS * u + h - 1)
                for s in range(SP):
                    for b in range(TG):
                        col = (SP * h + s) * P
                        last = nc.tensor.transpose(pT[:, h % 2, s, b * P:(b + 1) * P], r[:, c % C, b, col:col + P], ident[:])
                last.then_inc(part_T, 1)

            def aggregate(u, c):
                for h in range(2):
                    pe.wait_ge(e2_done, 2 * u + h + 1)
                    for s in range(HALF * h, HALF * (h + 1)):
                        k = SRC * c + s
                        last = nc.tensor.matmul(pAgg[:], msg[:, k], w[:, c % 2, s], start=(k == 0), stop=(k == K - 1))
                last.then_inc(agg_done, 1)

            def back(g):
                pe.wait_ge(aggT_copied, g + 1)
                if not isinstance(g, int) or g > 0:
                    pe.wait_ge(x2_done, g)
                for b in range(TG):
                    last = nc.tensor.transpose(pX[:, b], aggT[:, b * P:(b + 1) * P], ident[:])
                last.then_inc(x2_T, 1)

            pe.wait_ge(ident_ready, 1)
            for h in range(PARTS):
                part(0, 0, h)
            for h in range(2):
                part(1, 1, h)
            pe.wait_ge(dve_step, 8)
            for n in range(K // TG):
                if n >= 2:
                    pe.wait_ge(xnT_copied, n - 1)
                for b in range(TG):
                    last = nc.tensor.transpose(pM[:, n % 2, b], xn[:, TG * n + b], ident[:])
                last.then_inc(xn_T, 1)
            pe.wait_ge(wg_loaded, 16)
            for n in range(K // TG):
                pe.wait_ge(xnT_copied, min(n + 1 + 1, K // TG) if n < 2 else n + 1)
                if n < 2:
                    pe.wait_ge(xnT_copied, K // TG)
                if n >= 2:
                    pe.wait_ge(msg_ready, n - 1)
                for b in range(TG):
                    last = nc.tensor.matmul(pM[:, n % 2, b], xnT[:, TG * n + b], wg[:], start=True, stop=True)
                last.then_inc(msg_mm, 1)

            def transpose_xn2(g):
                pe.wait_ge(rows_ready, g + 1)
                for b in range(TG):
                    last = nc.tensor.transpose(pXn[:, b], rows[:, 0, b, 0:D], ident[:])
                last.then_inc(xn2_T, 1)

            def logits(g):
                pe.wait_ge(xn2T_copied, g + 1)
                if not isinstance(g, int) or g > 0:
                    pe.wait_ge(slots_ready, g)
                for b in range(TG):
                    last = nc.tensor.matmul(pLogits[:, b], xn2T[:, b * P:(b + 1) * P], rwT[:], start=True, stop=True)
                last.then_inc(logits_mm, 1)

            def rank(g):
                pe.wait_ge(picked, g + 1)
                M = lg[:, 4]
                nc.tensor.matmul(pRank, upper[:], M, start=True, stop=False, skip_group_check=True)
                for b in range(TG - 1):
                    nc.tensor.matmul(pRank[:, b + 1:], ones[:], M[:, b:b + 1].to_broadcast([P, TG - 1 - b, E]), start=False,
                                     stop=b == TG - 2, skip_group_check=True)
                for b in range(TG):
                    last = nc.tensor.matmul(pTot, ones[:], M[:, b], start=b == 0, stop=b == TG - 1, skip_group_check=True)
                last.then_inc(rank_mm, 1)

            def group(g, first=False, last=False):
                for c in range(C):
                    u = C * g + c
                    if not (last and c == C - 1):
                        for h in range(2, PARTS):
                            part(u + 1, c + 1, h)
                    if not (last and c >= C - 2):
                        for h in range(2):
                            part(u + 2, c + 2, h)
                    if first and c == 0:
                        pe.wait_ge(msg_ready, K // TG)
                    if not first:
                        if c == 0:
                            back(g - 1)
                        if c == 1:
                            transpose_xn2(g - 1)
                        if c == 2:
                            rank(g - 1)
                    aggregate(u, c)
                    if not first and c == 1:
                        logits(g - 1)
            pe.wait_ge(rw_loaded, 16)
            nc.tensor.transpose(pAgg[:, 0:E], rw[:], ident[0:E, 0:E]).then_inc(rw_T, 1)
            pe.wait_ge(rwT_copied, 1)
            group(0, first=True)
            group(1)
            with pe.Fori(2, G - 1) as g:
                group(g)
            group(G - 1, last=True)
            back(G - 1)
            transpose_xn2(G - 1)
            logits(G - 1)
            rank(G - 1)

            for n, (dst, rows_, lo, hi) in enumerate(weight_groups):
                if n == 0:
                    pe.wait_ge(ln_done, PARTS * U)
                    for m in range(5):
                        pe.wait_ge(w_loaded[m], 16)
                if n >= 4:
                    pe.wait_ge(w_copied, n - 3)
                if dst is not w2T:
                    raw = w1raw if dst is w1T else w3raw
                    for at in range(lo, hi, P):
                        m = min(P, hi - at)
                        last = nc.tensor.transpose(pW[n % 4][:, at - lo:at - lo + m], raw[0:m, at // P], ident[0:m, 0:m])
                else:
                    e = lo // (HT * D)
                    for at in range(lo, hi, D):
                        h0 = (at // D - HT * e) * P
                        last = nc.tensor.transpose(pW[n % 4][0:rows_, at - lo:at - lo + D], w2raw[:, e, h0:h0 + rows_], ident[:])
                last.then_inc(w_T, 1)

            def turn(t, i):
                if isinstance(t, int):
                    pe.wait_ge(xt_loaded[i % RING], 16 * (t // RING + 1))
                else:
                    pe.wait_ge(xt_loaded[i % RING], PER * (t - i % RING) + 16)
                if not isinstance(t, int) or t > 0:
                    pe.wait_ge(xtT_copied, t)
                nc.tensor.transpose(pXT, xt[:, i % RING, 0:D], ident[:]).then_inc(xt_T, 1)

            def up(t, i):
                pe.wait_ge(xtT_copied, t + 1)
                if not (isinstance(t, int) and t < 2):
                    pe.wait_ge(hid_ready, t - 1)
                pe.sem_inc(stood, 1)
                e = pe.value_load(tabi[0:1, 1, bass.ds(t, 1)], min_val=0, max_val=E - 1)
                nc.tensor.matmul(pH[i % 2][:, 0:H], xtT[:, i % 2], w1T[:, bass.ds(e * H, H)], start=True, stop=True)
                nc.tensor.matmul(pH[i % 2][:, 512:512 + H], xtT[:, i % 2], w3T[:, bass.ds(e * H, H)], start=True,
                                 stop=True).then_inc(h_mm, 1)

            def turn_hidden(t, i):
                pe.wait_ge(hid_ready, t + 1)
                if not isinstance(t, int) or t > 0:
                    pe.wait_ge(hidT_copied, t)
                for m in range(HT):
                    n = P if m < HT - 1 else HL
                    last = nc.tensor.transpose(pHT[0:n, m], hid[:, i % 2, m * P:m * P + n], ident[:])
                last.then_inc(hid_T, 1)

            def down(t, i):
                pe.wait_ge(hidT_copied, t + 1)
                if not isinstance(t, int) or t > 0:
                    pe.wait_ge(y_out, t)
                pe.sem_inc(stood, 1)
                e = pe.value_load(tabi[0:1, 1, bass.ds(t, 1)], min_val=0, max_val=E - 1)
                for m in range(HT):
                    n = P if m < HT - 1 else HL
                    last = nc.tensor.matmul(pY, hidT[0:n, i % 2, m], w2T[0:n, bass.ds(e * (HT * D) + m * D, D)],
                                            start=m == 0, stop=m == HT - 1)
                last.then_inc(y_mm, 1)

            def tile_pe(t, i):
                known = isinstance(t, int)
                if not known or t + 2 < TILES:
                    turn(t + 2, i + 2)
                if not known or t + 1 < TILES:
                    up(t + 1, i + 1)
                turn_hidden(t, i)
                if not known or t > 0:
                    down(t - 1, i + 1)

            pe.wait_ge(plan_ready, 1)
            pe.wait_ge(w_copied, len(weight_groups))
            turn(0, 0)
            turn(1, 1)
            up(0, 0)
            for t in range(RING):
                tile_pe(t, t)
            with pe.Fori(RING, TILES - RING, RING) as t:
                for i in range(RING):
                    tile_pe(t + i, i)
            for t in range(TILES - RING, TILES):
                tile_pe(t, t)
            down(TILES - 1, RING - 1)


_INS = ['x', 'adj', 'L0_gnn_W', 'L0_gnn_B', 'L0_ffn_router_w', 'L0_ffn_w1', 'L0_ffn_w2', 'L0_ffn_w3']
_OUTS = [((4096, 128), 'float32')]


def kernel(**inputs):
    import numpy as _np
    import concourse.bacc as _bacc
    from concourse import mybir as _mybir
    from concourse.bass_utils import run_bass_kernel_spmd as _run

    nc = _bacc.Bacc("TRN2", target_bir_lowering=False, num_devices=1)
    arrays, args = {}, []
    for name in _INS:
        a = _np.ascontiguousarray(inputs[name])
        arrays[f"in_{name}_dram"] = a
        args.append(nc.dram_tensor(f"in_{name}_dram", a.shape, _mybir.dt.from_np(a.dtype), kind="ExternalInput").ap())
    for i, (shape, dtype) in enumerate(_OUTS):
        dt = _mybir.dt.from_np(_np.dtype(dtype))
        args.append(nc.dram_tensor(f"out_{i}_dram", shape, dt, kind="ExternalOutput").ap())
    gnn_moe_layer(nc, *args)
    r = _run(nc, [arrays], core_ids=[0])
    return r.results[0]["out_0_dram"]
```

```python
import concourse.bass as bass
from concourse import mybir
from contextlib import ExitStack

F32 = mybir.dt.float32
BF16 = mybir.dt.bfloat16
U32 = mybir.dt.uint32
I32 = mybir.dt.int32
ALU = mybir.AluOpType
ACT = mybir.ActivationFunctionType
AX_X = mybir.AxisListType.X
P = 128
LN_EPS = 1e-5
TINY = 2.0 ** -60
TG = 4
SRC = 8


def gnn_moe_layer(nc, x, adjT, gnn_w, gnn_b, router_wT, w1_t, w2_t, w3_t, out):
    N, D = x.shape
    K = N // P
    G = K // TG
    C = K // SRC
    GW = TG * P
    HALF = SRC // 2
    U = G * C
    PAIRS = G // 2
    T2 = 2 * TG
    PU = 2 * C
    _, EH = w1_t.shape
    H, E, _ = w2_t.shape
    HT = -(-H // P)
    HL = H - (HT - 1) * P
    CAP = N + P
    TILES = 2 * N // P + E
    ROW = D + 2
    GB, IDB = D, D + 1
    FIRST = 2 * N * (PAIRS - 1) // PAIRS // P - E
    assert FIRST % 8 == 0
    RING = 8
    PER = 16 // RING
    assert TILES % RING == 0 and EH == E * H

    slots = nc.dram_tensor("slots", [E * CAP + E * P, ROW], F32, kind="Internal").ap()
    results = nc.dram_tensor("results", [2 * N + 2 * E * P, D], F32, kind="Internal").ap()

    x_v = x.rearrange("(k p) d -> p k d", p=P)
    out_v = out.rearrange("(k p) d -> p k d", p=P)

    with ExitStack() as ctx:
        def sb(name, shape, dt=F32):
            return ctx.enter_context(nc.sbuf_tensor(name, shape, dt))

        def pb(name, shape, dt=F32):
            return ctx.enter_context(nc.psum_tensor(name, shape, dt))

        def sem(name):
            return ctx.enter_context(nc.semaphore(name))

        r = sb("r", [P, C, SRC, GW])
        w = sb("w", [P, 2, SRC, GW])
        xs = sb("xs", [P, K, D])
        msg = sb("msg", [P, K, D])
        w2T = sb("w2T", [P, E * HT * D])
        shared = sb("shared", [P, 2, K * D])
        ident = sb("ident", [P, P])
        wg = sb("wg", [P, D])
        wc = sb("wc", [P, D])
        bg = sb("bg", [P, D])
        mean_op = sb("mean_op", [P, P])
        st1 = sb("st1", [P, 4, K])
        bn1 = sb("bn1", [P, K, 6])
        mv1 = sb("mv1", [P, K, 2])
        epsT = sb("epsT", [P, 2])
        bm2 = sb("bm2", [P, 1])
        upper = sb("upper", [P, P], BF16)
        ones = sb("ones", [P, P], BF16)
        rev = sb("rev", [P, E])
        ids = sb("ids", [P, K, 2], U32)
        pid = sb("pid", [P, E], I32)
        rows = sb("rows", [P, 2, T2, ROW])
        pad = sb("pad", [P, E, ROW])
        pad_at = sb("pad_at", [P, E], U32)
        pad_f = sb("pad_f", [P, E])
        rwT = sb("rwT", [P, E])
        bnst = sb("bnst", [P, TG, 6])
        mv = sb("mv", [P, 2, TG, 2])
        st2 = sb("st2", [P, 2, 4, TG])
        lg = sb("lg", [P, 8, T2, E])
        chosen = sb("chosen", [P, T2, E], BF16)
        sm = sb("sm", [P, 10, T2])
        soft = sb("soft", [P, T2 * E + T2])
        softe = sb("softe", [P, T2 * E + T2])
        base = sb("base", [P, E])
        slot_at = sb("slot_at", [P, T2, 2], U32)
        tau = sb("tau", [1, TILES])
        nt = sb("nt", [1, 8, E])
        nti = sb("nti", [1, 2, E], I32)
        tabi = sb("tabi", [1, 2, TILES + 2 * RING], I32)

        xT = shared[:, 0].rearrange("p (k d) -> p k d", d=D)
        w1T, w3T = shared[:, 0, 0:E * H], shared[:, 1, 0:E * H]
        aggT, xn2T = shared[:, 1, K * D - 2 * GW:K * D - GW], shared[:, 1, K * D - GW:]
        tab = shared[0:1, 0, E * H:E * H + TILES * E].rearrange("p (t e) -> p t e", e=E)
        tabf = shared[0:1, 0, E * H + TILES * E:E * H + TILES * (E + 3)].rearrange("p (a t) -> p a t", a=3)
        yf = r[:].rearrange("p a s n -> p (a s n)")
        xt = yf[:, 0:RING * ROW].rearrange("p (i n) -> p i n", n=ROW)
        at = RING * ROW
        xtT = yf[:, at:at + 2 * P].rearrange("p (i n) -> p i n", n=P)
        at += 2 * P
        sil = yf[:, at:at + 2 * HT * P].rearrange("p (i n) -> p i n", n=HT * P)
        at += 2 * HT * P
        hid = yf[:, at:at + 2 * HT * P].rearrange("p (i n) -> p i n", n=HT * P)
        at += 2 * HT * P
        hidT = yf[:, at:at + 2 * HT * P].rearrange("p (i j n) -> p i j n", j=HT, n=P)
        at += 2 * HT * P
        yo = yf[:, at:at + RING * D].rearrange("p (i n) -> p i n", n=D)
        res = w[:].rearrange("p a s n -> p (a s n)").rearrange("p (k c d) -> p k c d", c=2, d=D)

        pH_ = pb("pH_", [P, 2, 2, GW])
        pAgg = pb("pAgg", [P, GW])
        pX = pb("pX", [P, TG, P])
        pXn = pb("pXn", [P, TG, P])
        pSm = pb("pSm", [P, GW])
        pLogits = pSm[:, 0:T2 * E].rearrange("p (b e) -> p b e", e=E)
        pRank = pSm[:, 128:128 + T2 * E].rearrange("p (b e) -> p b e", e=E)
        pTot = pSm[:, 256:256 + E]
        pPost = pX[:].rearrange("p b d -> p (b d)")
        pLogits_last = pPost[:, 0:TG * E].rearrange("p (b e) -> p b e", e=E)
        pRank_last = pPost[:, 128:128 + T2 * E].rearrange("p (b e) -> p b e", e=E)
        pTot_last = pPost[:, 256:256 + E]
        pP = [pH_[:, n // 2, n % 2].rearrange("p (b d) -> p b d", d=D) for n in range(4)]
        pH = [pH_[:, 0].rearrange("p s n -> p (s n)"), pH_[:, 1].rearrange("p s n -> p (s n)")]
        pHT = pXn[:, 0:HT]
        pXT = pAgg[:, 0:P]
        pY = pSm[:, 0:D]

        first_half = sem("first_half")
        r_loaded = [sem(f"r_loaded{c}") for c in range(C)]
        x_loaded, wg_loaded, bg_loaded, rw_loaded = sem("x_loaded"), sem("wg_loaded"), sem("bg_loaded"), sem("rw_loaded")
        w_loaded = [sem(f"w_loaded{n}") for n in range(2 + HT)]
        id0, ident_ready, consts_ready, ops_ready = sem("id0"), sem("ident_ready"), sem("consts_ready"), sem("ops_ready")
        masked, ln_done, e1_done, q_done, e2_done, agg_done = (sem("masked"), sem("ln_done"), sem("e1_done"),
                                                             sem("q_done"), sem("e2_done"), sem("agg_done"))
        colmean_mm, wc_ready = sem("colmean_mm"), sem("wc_ready")
        x_T, xT_copied, msg_mm, msg_ready = sem("x_T"), sem("xT_copied"), sem("msg_mm"), sem("msg_ready")
        bn1_done, var1_ready, ln1_act, newton1 = sem("bn1_done"), sem("var1_ready"), sem("ln1_act"), sem("newton1")
        aggT_copied, x2_T, x2_done = sem("aggT_copied"), sem("x2_T"), sem("x2_done")
        bn2_done, var2_ready, ln2_act, newton2, rstd2_ready = (sem("bn2_done"), sem("var2_ready"), sem("ln2_act"),
                                                               sem("newton2"), sem("rstd2_ready"))
        centred2, xn2_ready, xn2_copied, ids_placed = sem("centred2"), sem("xn2_ready"), sem("xn2_copied"), sem("ids_placed")
        xn2_T, xn2T_copied, logits_mm = sem("xn2_T"), sem("xn2T_copied"), sem("logits_mm")
        route = sem("route")
        soft_in, soft_done, picked, rank_mm, slots_ready = (sem("soft_in"), sem("soft_done"), sem("picked"),
                                                            sem("rank_mm"), sem("slots_ready"))
        tables_ready, pad_zeroed, pad_ids = sem("tables_ready"), sem("pad_zeroed"), sem("pad_ids")
        scattered, padded, dummies_stored = sem("scattered"), sem("padded"), sem("dummies_stored")
        plan, plan1_ready, plan2_ready, logits_copied = sem("plan"), sem("plan1_ready"), sem("plan2_ready"), sem("logits_copied")
        xt_loaded = [sem(f"xt_loaded{i}") for i in range(RING)]
        yt_stored = [sem(f"yt_stored{i}") for i in range(RING)]
        xt_T, xtT_copied, h_mm, sil_done, hid_ready, hid_T, hidT_copied, y_mm, y_out = (
            sem("xt_T"), sem("xtT_copied"), sem("h_mm"), sem("sil_done"), sem("hid_ready"), sem("hid_T"),
            sem("hidT_copied"), sem("y_mm"), sem("y_out"))
        res_loaded = [sem(f"res_loaded{n}") for n in range(4)]
        res_added, out_stored = sem("res_added"), sem("out_stored")
        stood = sem("stood")
        NC = 4
        KC = K // NC
        NEWTON_AT, XN_AT, COPY_AT, LOGITS_AT, PICK_AT, RANK_AT, PLACE_AT, PLAN_AT = 0, 2, 3, 4, 5, 6, 7, 8
        SCATTER_AT = PLACE_AT + 1
        PEEL = 2 * RING
        PEEL2 = RING * (-(-(SCATTER_AT + 2 * T2 + E) // RING))
        BODY = 2 * RING
        assert PLAN_AT < PEEL and PEEL2 <= FIRST and (TILES - PEEL - RING) % BODY == 0
        STORE = 16 * 2 * T2

        def tiles_of(g):
            return slice(TG * g, TG * g + TG) if isinstance(g, int) else bass.ds(TG * g, TG)

        def known(t):
            return isinstance(t, int)

        block = ctx.enter_context(nc.Block())

        def load_at(sp, t, i):
            at = sp.value_load(tabi[0:1, 0, bass.ds(t, 1)], min_val=0, max_val=E * CAP + (E - 1) * P)
            sp.dma_start(xt[:, i], slots[bass.ds(at, P), :]).then_inc(xt_loaded[i], 16)

        def reload_ring(sp, t):
            for i in range(RING):
                sp.wait_ge(yt_stored[i], PER * t)
                sp.sem_inc(stood, 1)
                load_at(sp, t + i, i)

        @block.sync
        def _(sp):
            def load(g, c):
                sp.dma_start(r[:, c].rearrange("p s n -> p (s n)"), adjT[g, c]).then_inc(r_loaded[c], 16)

            sp.dma_start(r[:, 0, 0:HALF].rearrange("p s n -> p (s n)"), adjT[0, 0, :, 0:HALF * GW]).then_inc(first_half, 16)
            sp.dma_start(r[:, 0, HALF:].rearrange("p s n -> p (s n)"), adjT[0, 0, :, HALF * GW:]).then_inc(r_loaded[0], 16)
            sp.dma_start(wg[:], gnn_w).then_inc(wg_loaded, 16)
            load(0, 1)
            sp.dma_start(xs[:], x_v).then_inc(x_loaded, 16)
            sp.dma_start(bg[:], gnn_b.rearrange("(a d) -> a d", a=1).to_broadcast([P, D])).then_inc(bg_loaded, 16)
            for c in range(2, C):
                load(0, c)
            sp.dma_start(rwT[:], router_wT).then_inc(rw_loaded, 16)
            for c in range(C):
                sp.wait_ge(e2_done, c + 1)
                load(1, c)
            sp.wait_ge(msg_ready, K)
            sp.dma_start(w1T, w1_t).then_inc(w_loaded[0], 16)
            sp.dma_start(w3T, w3_t).then_inc(w_loaded[1], 16)
            w2v = w2T[:].rearrange("p (e m d) -> p e m d", m=HT, d=D)
            for m in range(HT):
                n = P if m < HT - 1 else HL
                sp.dma_start(w2v[0:n, :, m], w2_t[m * P:m * P + n]).then_inc(w_loaded[2 + m], 16)
            with sp.Fori(2, G) as g:
                for c in range(C):
                    sp.wait_ge(e2_done, C * g + c - C + 1)
                    load(g, c)

            sp.wait_ge(plan1_ready, 1)
            sp.wait_ge(scattered, STORE * (PAIRS - 1))
            sp.wait_ge(e2_done, U - 2)
            for i in range(RING):
                load_at(sp, i, i)
            with sp.Fori(RING, FIRST, RING) as t:
                reload_ring(sp, t)
            sp.wait_ge(plan2_ready, 1)
            sp.wait_ge(dummies_stored, 16)
            sp.wait_ge(padded, 16 * E)
            sp.wait_ge(scattered, STORE * PAIRS)
            with sp.Fori(FIRST, TILES, RING) as t:
                reload_ring(sp, t)
            for i in range(RING):
                sp.wait_ge(yt_stored[i], 16 * (TILES // RING))
            rv = results[0:2 * N].rearrange("(k p c) d -> p k c d", p=P, c=2)
            for n in range(NC):
                sp.dma_start(res[:, KC * n:KC * n + KC], rv[:, KC * n:KC * n + KC]).then_inc(res_loaded[n], 16)
            for n in range(NC):
                sp.wait_ge(res_added, 2 * n + 2)
                sp.dma_start(out_v[:, KC * n:KC * n + KC], xs[:, KC * n:KC * n + KC]).then_inc(out_stored, 16)
            sp.wait_ge(out_stored, 16 * NC)

        @block.gpsimd
        def _(pool):
            nc.gpsimd.memset(epsT[:, 0:1], TINY)
            nc.gpsimd.memset(bm2[:], -2.0)
            nc.gpsimd.memset(epsT[:, 1:2], LN_EPS).then_inc(consts_ready, 1)
            nc.gpsimd.memset(ident[:], 0.0).then_inc(id0, 1)
            pool.wait_ge(id0, 1)
            nc.gpsimd.affine_select(out=ident[:], in_=ident[:], compare_op=ALU.not_equal, fill=1.0, base=0,
                                    pattern=[[-1, P]], channel_multiplier=1).then_inc(ident_ready, 1)
            nc.gpsimd.memset(mean_op[:], 1.0 / D).then_inc(ops_ready, 1)
            nc.gpsimd.memset(ones[:], 1.0).then_inc(id0, 1)
            pool.wait_ge(id0, 2)
            nc.gpsimd.affine_select(out=upper[:], in_=ones[:], compare_op=ALU.is_gt, fill=0.0, base=0,
                                    pattern=[[1, P]], channel_multiplier=-1)
            nc.gpsimd.iota(ids[:], [[2 * P, K], [1, 2]], base=0, channel_multiplier=2)
            nc.gpsimd.iota(pid[:], [[0, E]], base=0, channel_multiplier=1)
            nc.gpsimd.iota(rev[:], [[-1, E]], base=E, channel_multiplier=0, allow_small_or_imprecise_dtypes=True)
            nc.gpsimd.iota(base[:], [[CAP, E]], base=0, channel_multiplier=0, allow_small_or_imprecise_dtypes=True)
            nc.gpsimd.iota(tau[:], [[1, TILES]], base=0, channel_multiplier=0,
                           allow_small_or_imprecise_dtypes=True).then_inc(tables_ready, 1)
            pool.wait_ge(tables_ready, 1)
            nc.gpsimd.memset(pad[:], 0.0).then_inc(pad_zeroed, 1)
            pool.wait_ge(pad_zeroed, 1)
            nc.gpsimd.iota(pad[:, :, IDB:IDB + 1].bitcast(U32), [[P, E], [0, 1]], base=2 * N + E * P,
                           channel_multiplier=1).then_inc(pad_ids, 1)
            pool.wait_ge(pad_ids, 1)
            pool.dma_start(slots[E * CAP:E * CAP + E * P].rearrange("(e p) n -> p e n", p=P),
                           pad[:]).then_inc(dummies_stored, 16)
            pool.wait_ge(dummies_stored, 16)
            nc.gpsimd.iota(pad[:, :, IDB:IDB + 1].bitcast(U32), [[P, E], [0, 1]], base=2 * N,
                           channel_multiplier=1).then_inc(pad_ids, 1)

            def normalise(g, h, pr):
                if h == 0 and not (known(pr) and pr == 0):
                    pool.wait_ge(scattered, STORE * pr)
                pool.wait_ge(rstd2_ready, g + 1)
                a, b = rows[:, 0, TG * h:TG * h + TG, 0:D], rows[:, 1, TG * h:TG * h + TG, 0:D]
                nc.gpsimd.tensor_tensor(b, xs[:, tiles_of(g)], mv[:, h, :, 0:1].to_broadcast([P, TG, D]),
                                        ALU.subtract).then_inc(centred2, 1)
                pool.wait_ge(centred2, g + 1)
                nc.gpsimd.tensor_tensor(a, b, st2[:, h, 2].unsqueeze(2).to_broadcast([P, TG, D]),
                                        ALU.mult).then_inc(xn2_ready, 1)
                pool.wait_ge(xn2_ready, g + 1)
                pool.sem_inc(stood, 1)
                nc.gpsimd.tensor_copy(b, a).then_inc(xn2_copied, 1)

            def scatter_tile(b, ch):
                pool.indirect_dma_start(slots, bass.IndirectOffsetOnAxis(slot_at[:, b, ch:ch + 1], 0),
                                        rows[:, ch, b], None).then_inc(scattered, 16)

            def number(pr):
                for ch in range(2):
                    nc.gpsimd.tensor_copy(rows[:, ch, :, IDB:IDB + 1].bitcast(U32),
                                          ids[:, slice(T2 * pr, T2 * pr + T2) if known(pr) else bass.ds(T2 * pr, T2),
                                              ch:ch + 1]).then_inc(ids_placed, 1)
                pool.wait_ge(ids_placed, 2 * pr + 2)
                pool.wait_ge(xn2_copied, 2 * pr + 2)
                pool.wait_ge(slots_ready, pr + 1)
                pool.sem_inc(stood, 1)
            normalise(0, 0, 0)
            with pool.Fori(1, PAIRS) as pr:
                normalise(2 * pr - 1, 1, pr - 1)
                number(pr - 1)
                for b in range(T2):
                    for ch in range(2):
                        scatter_tile(b, ch)
                normalise(2 * pr, 0, pr)

            def store_tile(t, i):
                pool.wait_ge(y_out, t + 1)
                pool.sem_inc(stood, 1)
                pool.indirect_dma_start(results, bass.IndirectOffsetOnAxis(xt[:, i, IDB:IDB + 1].bitcast(U32), 0),
                                        yo[:, i], None).then_inc(yt_stored[i], 16)

            normalise(G - 1, 1, PAIRS - 1)
            for t in range(PEEL2):
                store_tile(t, t % RING)
                n = t - SCATTER_AT
                if n == 0:
                    number(PAIRS - 1)
                if 0 <= n < 2 * T2:
                    scatter_tile(n // 2, n % 2)
                if n == 2 * T2:
                    pool.wait_ge(plan2_ready, 1)
                    pool.wait_ge(pad_ids, 2)
                if 2 * T2 <= n < 2 * T2 + E:
                    e = n - 2 * T2
                    pool.indirect_dma_start(slots, bass.IndirectOffsetOnAxis(pad_at[:, e:e + 1], 0), pad[:, e],
                                            None).then_inc(padded, 16)
            with pool.Fori(PEEL2, TILES, RING) as t:
                for i in range(RING):
                    store_tile(t + i, i)

        @block.scalar
        def _(act):
            def ln(u, c):
                act.wait_ge(masked, u + 2)
                nc.scalar.activation(r[:, c], r[:, c], ACT.Ln, bias=epsT[:, 0:1]).then_inc(ln_done, 1)

            def inverse(u, c):
                act.wait_ge(ln_done, u + 2)
                nc.scalar.activation(r[:, c], r[:, c], ACT.Exp, scale=-1.0).then_inc(e1_done, 1)

            def weigh(u, c):
                act.wait_ge(q_done, u + 1)
                if not (known(u) and u < 2):
                    act.wait_ge(agg_done, u - 1)
                nc.scalar.activation(w[:, c % 2], r[:, c], ACT.Exp, scale=-2.0, bias=bm2[:, 0:1]).then_inc(e2_done, 1)

            def rstd2(g, h):
                act.wait_ge(var2_ready, g + 1)
                if not (known(g) and g < 2):
                    act.wait_ge(rstd2_ready, g - 1)
                nc.scalar.activation(st2[:, h, 0], mv[:, h, :, 1], ACT.Ln, bias=epsT[:, 1:2]).then_inc(ln2_act, 1)
                act.wait_ge(ln2_act, 2 * g + 1)
                nc.scalar.activation(st2[:, h, 1], st2[:, h, 0], ACT.Exp, scale=-0.5).then_inc(ln2_act, 1)

            def softmax_exp(pr):
                act.wait_ge(soft_in, pr + 1)
                nc.scalar.activation(softe[:], soft[:], ACT.Exp).then_inc(soft_done, 1)

            def steps(pr, first=False, last=False):
                for j in range(PU):
                    u, c = PU * pr + j, j % C
                    ahead = not (last and j == PU - 1)
                    if ahead:
                        ln(u + 1, (c + 1) % C)
                    if j == 2 and not first:
                        rstd2(2 * pr - 1, 1)
                    if j == 5 and not first:
                        softmax_exp(pr - 1)
                    if j == 7:
                        rstd2(2 * pr, 0)
                    if ahead:
                        inverse(u + 1, (c + 1) % C)
                    weigh(u, c)
                    if first and j == 1:
                        act.wait_ge(var1_ready, 1)
                        nc.scalar.activation(st1[:, 0], mv1[:, :, 1], ACT.Ln, bias=epsT[:, 1:2]).then_inc(ln1_act, 1)
                        act.wait_ge(ln1_act, 1)
                        nc.scalar.activation(st1[:, 1], st1[:, 0], ACT.Exp, scale=-0.5).then_inc(ln1_act, 1)
                    if first and j == 0:
                        for n in range(K // TG):
                            act.wait_ge(x_T, n + 1)
                            nc.scalar.activation(xT[:, TG * n:TG * n + TG], pP[n % 4], ACT.Copy).then_inc(xT_copied, 1)

            act.wait_ge(consts_ready, 1)
            nc.scalar.preload_act_table_set("natural_log_exp_and_others")
            for h in range(2):
                act.wait_ge(masked, h + 1)
                v = r[:, 0, HALF * h:HALF * h + HALF]
                nc.scalar.activation(v, v, ACT.Ln, bias=epsT[:, 0:1]).then_inc(ln_done, 1)
            inverse(0, 0)
            steps(0, first=True)
            with act.Fori(1, PAIRS - 1) as pr:
                steps(pr)
            steps(PAIRS - 1, last=True)
            def silu(t, i):
                act.wait_ge(h_mm, t + 1)
                if not (isinstance(t, int) and t < 2):
                    act.wait_ge(hid_ready, t - 1)
                nc.scalar.activation(sil[:, i % 2, 0:H], pH[i % 2][:, 0:H], ACT.Silu).then_inc(sil_done, 1)

            def copy_hidT(t, i):
                act.wait_ge(hid_T, t + 1)
                if not (isinstance(t, int) and t < 2):
                    act.wait_ge(y_mm, t - 1)
                nc.scalar.activation(hidT[:, i % 2, 0:HT - 1], pHT[:, 0:HT - 1], ACT.Copy)
                nc.scalar.activation(hidT[0:HL, i % 2, HT - 1], pHT[0:HL, HT - 1], ACT.Copy).then_inc(hidT_copied, 1)

            def tile_act(t, i):
                if known(t) and t == RANK_AT:
                    softmax_exp(PAIRS - 1)
                if not known(t) or t + 1 < TILES:
                    silu(t + 1, i + 1)
                copy_hidT(t, i)

            rstd2(G - 1, 1)
            silu(0, 0)
            for t in range(PEEL):
                tile_act(t, t)
            with act.Fori(PEEL, TILES - RING, RING) as t:
                for i in range(RING):
                    tile_act(t + i, i)
            for t in range(TILES - RING, TILES):
                tile_act(t, t)

        @block.vector
        def _(dve):
            def masking(v):
                nc.vector.scalar_tensor_tensor(out=v, in0=v, scalar=1.0, in1=v, op0=ALU.is_lt,
                                               op1=ALU.mult).then_inc(masked, 1)

            def mask(g, c):
                dve.wait_ge(r_loaded[c], 16 * (g + 1))
                masking(r[:, c])

            def exponent(u, c):
                dve.wait_ge(e1_done, u + 1)
                nc.vector.scalar_tensor_tensor(out=r[:, c], in0=r[:, c], scalar=2.0, in1=r[:, c], op0=ALU.subtract,
                                               op1=ALU.mult).then_inc(q_done, 1)

            def copy_aggT(g):
                dve.wait_ge(agg_done, C * (g + 1))
                if not (known(g) and g == 0):
                    dve.wait_ge(x2_T, g)
                nc.vector.tensor_copy(aggT, pAgg[:]).then_inc(aggT_copied, 1)

            def add_x(g):
                dve.wait_ge(x2_T, g + 1)
                nc.vector.tensor_tensor(xs[:, tiles_of(g)], pX[:], xs[:, tiles_of(g)], ALU.add).then_inc(x2_done, 1)

            def moments(g, h):
                dve.wait_ge(x2_done, g + 1)
                if not (known(g) and g < 2):
                    dve.wait_ge(xn2_ready, g - 1)
                dve.sem_inc(stood, 1)
                for b in range(TG):
                    v = xs[:, TG * g + b] if known(g) else xs[:, bass.ds(TG * g + b, 1)].rearrange("p a d -> p (a d)")
                    nc.vector.bn_stats(bnst[:, b], v).then_inc(bn2_done, 1)
                dve.wait_ge(bn2_done, TG * (g + 1))
                dve.sem_inc(stood, 1)
                for b in range(TG):
                    last = nc.vector.bn_aggr(mv[:, h, b], bnst[:, b])
                last.then_inc(var2_ready, 1)

            def newton(g, h):
                dve.wait_ge(ln2_act, 2 * g + 2)
                s = st2[:, h]
                nc.vector.tensor_scalar(s[:, 2], mv[:, h, :, 1], -0.5, -0.5 * LN_EPS, ALU.mult, ALU.add).then_inc(newton2, 1)
                nc.vector.tensor_tensor(s[:, 3], s[:, 1], s[:, 1], ALU.mult).then_inc(newton2, 1)
                dve.wait_ge(newton2, 3 * g + 2)
                nc.vector.tensor_tensor(s[:, 3], s[:, 3], s[:, 2], ALU.mult).then_inc(newton2, 1)
                dve.wait_ge(newton2, 3 * g + 3)
                nc.vector.scalar_tensor_tensor(out=s[:, 2], in0=s[:, 3], scalar=1.5, in1=s[:, 1], op0=ALU.add,
                                               op1=ALU.mult).then_inc(rstd2_ready, 1)

            def copy_xn2T(g, bank=None):
                dve.wait_ge(xn2_T, g + 1)
                if not (known(g) and g == 0):
                    dve.wait_ge(logits_mm, g)
                nc.vector.tensor_copy(xn2T, pXn[:].rearrange("p b d -> p (b d)") if bank is None else bank).then_inc(
                    xn2T_copied, 1)

            def bc(v):
                return v.unsqueeze(2).to_broadcast([P, T2, E])

            revb = rev[:].unsqueeze(1).to_broadcast([P, T2, E])
            PICK, STEPS = 11, 26

            class Steps:
                def __init__(self, pr, n):
                    self.pr, self.n = pr, n

                def __call__(self, ins):
                    ins.then_inc(route, 1)
                    self.n += 1

                def after(self):
                    dve.wait_ge(route, STEPS * self.pr + self.n)

            def pick(pr, last=False):
                dve.wait_ge(logits_mm, 2 * pr + 2)
                do = Steps(pr, 0)
                L, A, B, t0 = lg[:, 0], lg[:, 1], lg[:, 2], lg[:, 3]
                if last:
                    do(nc.vector.tensor_copy(L[:, TG:], pLogits_last))
                else:
                    do(nc.vector.tensor_copy(L, pLogits))
                for n, (src, one_hot) in enumerate(((L, A), (lg[:, 5], B))):
                    do.after()
                    if n:
                        do(nc.vector.scalar_tensor_tensor(out=src, in0=A, scalar=-3.0e38, in1=L, op0=ALU.mult, op1=ALU.add))
                        do.after()
                    do(nc.vector.reduce_max(sm[:, n], src, AX_X))
                    do.after()
                    do(nc.vector.tensor_tensor(t0, src, bc(sm[:, n]), ALU.is_equal))
                    do.after()
                    do(nc.vector.tensor_tensor(t0, t0, revb, ALU.mult))
                    do.after()
                    do(nc.vector.reduce_max(sm[:, 2], t0, AX_X))
                    do.after()
                    if n == 0:
                        do(nc.vector.tensor_tensor(one_hot, t0, bc(sm[:, 2]), ALU.is_equal))
                nc.vector.tensor_tensor(B, t0, bc(sm[:, 2]), ALU.is_equal).then_inc(picked, 1)
                nc.vector.tensor_tensor(soft[:, 0:T2 * E].rearrange("p (b e) -> p b e", e=E), L, bc(sm[:, 0]), ALU.subtract)
                nc.vector.tensor_tensor(soft[:, T2 * E:], sm[:, 1], sm[:, 0], ALU.subtract).then_inc(soft_in, 1)
                dve.wait_ge(picked, 2 * pr + 1)
                nc.vector.tensor_tensor(chosen[:], A, B, ALU.add).then_inc(picked, 1)
                assert do.n == PICK, do.n

            def place(pr, pRank=pRank, pTot=pTot):
                do = Steps(pr, PICK)
                A, B, V, VA, VB = lg[:, 1], lg[:, 2], lg[:, 3], lg[:, 6], lg[:, 7]
                dve.wait_ge(rank_mm, pr + 1)
                do(nc.vector.tensor_tensor(V, pRank, base[:].unsqueeze(1).to_broadcast([P, T2, E]), ALU.add))
                do.after()
                do(nc.vector.tensor_tensor(VA, V, A, ALU.mult))
                do(nc.vector.tensor_tensor(VB, V, B, ALU.mult))
                do(nc.vector.tensor_tensor(base[:], pTot, base[:], ALU.add))
                do.after()
                do(nc.vector.reduce_sum(sm[:, 3], VA, AX_X))
                do(nc.vector.reduce_sum(sm[:, 4], VB, AX_X))
                dve.wait_ge(soft_done, pr + 1)
                do(nc.vector.reduce_sum(sm[:, 5], softe[:, 0:T2 * E].rearrange("p (b e) -> p b e", e=E), AX_X))
                do.after()
                do(nc.vector.tensor_copy(slot_at[:, :, 0], sm[:, 3]))
                do(nc.vector.tensor_copy(slot_at[:, :, 1], sm[:, 4]))
                do(nc.vector.reciprocal(sm[:, 6], sm[:, 5]))
                do.after()
                do(nc.vector.tensor_tensor(sm[:, 7], softe[:, T2 * E:], sm[:, 6], ALU.mult))
                do.after()
                do(nc.vector.tensor_tensor(sm[:, 8], sm[:, 6], sm[:, 7], ALU.add))
                do.after()
                do(nc.vector.tensor_scalar(sm[:, 8], sm[:, 8], 1e-9, None, ALU.add))
                do.after()
                do(nc.vector.reciprocal(sm[:, 9], sm[:, 8]))
                do.after()
                do(nc.vector.tensor_tensor(rows[:, 0, :, GB], sm[:, 6], sm[:, 9], ALU.mult))
                nc.vector.tensor_tensor(rows[:, 1, :, GB], sm[:, 7], sm[:, 9], ALU.mult).then_inc(slots_ready, 1)
                assert do.n == STEPS, do.n

            def steps(pr, first=False, last=False):
                for j in range(PU):
                    u, c = PU * pr + j, j % C
                    if first and j == 2:
                        messages(0)
                    exponent(u, c)
                    if first and j == 0:
                        dve.wait_ge(x_loaded, 16)
                        for k in range(K):
                            nc.vector.bn_stats(bn1[:, k], xs[:, k]).then_inc(bn1_done, 1)
                        mask(0, 2)
                    if first and j == 1:
                        mask(0, 3)
                        dve.wait_ge(bn1_done, K)
                        for k in range(K):
                            ins = nc.vector.bn_aggr(mv1[:, k], bn1[:, k])
                        ins.then_inc(var1_ready, 1)
                        newton1_step()
                    if j == 1 and not first:
                        add_x(2 * pr - 1)
                        moments(2 * pr - 1, 1)
                    if j == 6:
                        add_x(2 * pr)
                        moments(2 * pr, 0)
                    if not (last and j >= PU - 2) and not (first and j < 2):
                        mask(2 * pr + (j + 2) // C, (j + 2) % C)
                    if first and j == 2:
                        messages(1)
                    if first and j == 3:
                        for n in range(2, C):
                            messages(n)
                    if not first:
                        if j == 0:
                            copy_aggT(2 * pr - 1)
                        if j == 1:
                            copy_xn2T(2 * pr - 2)
                        if j == 2:
                            newton(2 * pr - 1, 1)
                        if j == 3:
                            copy_xn2T(2 * pr - 1)
                    if j == 4:
                        copy_aggT(2 * pr)
                    if not first:
                        if j == 4:
                            pick(pr - 1)
                        if j == 5:
                            place(pr - 1)
                    if j == 7:
                        newton(2 * pr, 0)

            def newton1_step():
                dve.wait_ge(ln1_act, 2)
                s = st1
                nc.vector.tensor_scalar(s[:, 2], mv1[:, :, 1], -0.5, -0.5 * LN_EPS, ALU.mult, ALU.add).then_inc(newton1, 1)
                nc.vector.tensor_tensor(s[:, 3], s[:, 1], s[:, 1], ALU.mult).then_inc(newton1, 1)
                dve.wait_ge(newton1, 2)
                nc.vector.tensor_tensor(s[:, 3], s[:, 3], s[:, 2], ALU.mult).then_inc(newton1, 1)
                dve.wait_ge(newton1, 3)
                nc.vector.scalar_tensor_tensor(out=s[:, 2], in0=s[:, 3], scalar=1.5, in1=s[:, 1], op0=ALU.add,
                                               op1=ALU.mult).then_inc(newton1, 1)

            def messages(c):
                if c == 0:
                    dve.wait_ge(newton1, 4)
                    dve.wait_ge(bg_loaded, 16)
                for k in range(SRC * c, SRC * c + SRC):
                    if k % TG == 0:
                        dve.wait_ge(msg_mm, k // TG + 1)
                    nc.vector.scalar_tensor_tensor(out=msg[:, k], in0=pP[k // TG % 4][:, k % TG], scalar=st1[:, 2, k:k + 1],
                                                   in1=bg[:], op0=ALU.mult, op1=ALU.add).then_inc(msg_ready, 1)

            dve.wait_ge(first_half, 16)
            masking(r[:, 0, 0:HALF])
            dve.wait_ge(r_loaded[0], 16)
            masking(r[:, 0, HALF:])
            dve.wait_ge(colmean_mm, 1)
            nc.vector.tensor_tensor(wc[:], wg[:], pSm[:, 0:D], ALU.subtract).then_inc(wc_ready, 1)
            mask(0, 1)
            steps(0, first=True)
            dve.wait_ge(tables_ready, 1)
            with dve.Fori(1, PAIRS - 1) as pr:
                steps(pr)
            steps(PAIRS - 1, last=True)
            class Links:
                n = 0

                def __call__(self, ins):
                    ins.then_inc(plan, 1)
                    self.n += 1
                    dve.wait_ge(plan, self.n)

            link = Links()
            CNT, NT, CUM, SKIP, D1 = 0, 1, 2, 3, 4

            def plan_tiles(lo, n, done):
                if done:
                    link(nc.vector.tensor_tensor(pad_f[:], base[:], pid[:], ALU.add))
                    link(nc.vector.tensor_copy(pad_at[:], pad_f[:]))
                link(nc.vector.scalar_tensor_tensor(out=nt[:, CNT], in0=rev[0:1, :], scalar=float(CAP), in1=base[0:1, :],
                                                    op0=ALU.mult, op1=ALU.add))
                link(nc.vector.tensor_scalar(nti[:, 0], nt[:, CNT], float((P - 1 if done else 0) - E * CAP), None, ALU.add))
                link(nc.vector.tensor_scalar(nti[:, 1], nti[:, 0], P.bit_length() - 1, None, ALU.logical_shift_right))
                link(nc.vector.tensor_copy(nt[:, NT], nti[:, 1]))
                link(nc.vector.tensor_scalar(nt[:, SKIP], nt[:, NT], -float(P), float(CAP), ALU.mult, ALU.add))
                if done:
                    link(nc.vector.scalar_tensor_tensor(out=nt[:, SKIP, 0:E - 1], in0=nt[:, D1, 1:E], scalar=float(P),
                                                        in1=nt[:, SKIP, 0:E - 1], op0=ALU.mult, op1=ALU.add))
                    link(nc.vector.tensor_tensor(nt[:, NT], nt[:, NT], nt[:, D1], ALU.subtract))
                link(nc.vector.tensor_copy(nt[:, CUM, 0:1], nt[:, NT, 0:1]))
                for e in range(1, E):
                    link(nc.vector.tensor_tensor(nt[:, CUM, e:e + 1], nt[:, CUM, e - 1:e], nt[:, NT, e:e + 1], ALU.add))
                tb = tau[:, 0:n].unsqueeze(2).to_broadcast([1, n, E])
                link(nc.vector.tensor_tensor(tab[:, 0:n], tb, nt[:, CUM:CUM + 1].to_broadcast([1, n, E]), ALU.is_ge))
                link(nc.vector.reduce_sum(tabf[:, 0, 0:n], tab[:, 0:n], AX_X))
                link(nc.vector.tensor_scalar(tabi[:, 1, lo:lo + n], tabf[:, 0, 0:n], float(E - 1), None, ALU.min))
                link(nc.vector.tensor_tensor(tab[:, 0:n], tab[:, 0:n], nt[:, SKIP:SKIP + 1].to_broadcast([1, n, E]), ALU.mult))
                link(nc.vector.reduce_sum(tabf[:, 1, 0:n], tab[:, 0:n], AX_X))
                link(nc.vector.scalar_tensor_tensor(out=tabf[:, 2, 0:n], in0=tau[:, 0:n], scalar=float(P),
                                                    in1=tabf[:, 1, 0:n], op0=ALU.mult, op1=ALU.add))
                if done:
                    link(nc.vector.scalar_tensor_tensor(out=tabf[:, 0, 0:n], in0=nt[:, D1, 0:1].to_broadcast([1, n]),
                                                        scalar=float(P), in1=tabf[:, 2, 0:n], op0=ALU.mult, op1=ALU.add))
                else:
                    link(nc.vector.tensor_scalar(nt[:, CNT], nt[:, CUM], float(n), None, ALU.min))
                    link(nc.vector.tensor_copy(nt[:, D1, 0:1], nt[:, CNT, 0:1]))
                    link(nc.vector.tensor_tensor(nt[:, D1, 1:E], nt[:, CNT, 1:E], nt[:, CNT, 0:E - 1], ALU.subtract))
                nc.vector.tensor_copy(tabi[:, 0, lo:lo + n], tabf[:, 0 if done else 2, 0:n]).then_inc(
                    plan2_ready if done else plan1_ready, 1)

            def copy_xt(t, i):
                dve.wait_ge(xt_T, t + 1)
                if not (isinstance(t, int) and t < 2):
                    dve.wait_ge(h_mm, t - 1)
                nc.vector.tensor_copy(xtT[:, i % 2], pXT).then_inc(xtT_copied, 1)

            def gated(t, i):
                dve.wait_ge(y_mm, t + 1)
                if not (isinstance(t, int) and t < RING):
                    dve.wait_ge(yt_stored[i % RING], 16 * (t // RING) if isinstance(t, int) else PER * (t - i % RING))
                nc.vector.tensor_scalar(yo[:, i % RING], pY, xt[:, i % RING, GB:GB + 1], None, ALU.mult).then_inc(y_out, 1)

            def hidden(t, i):
                dve.wait_ge(sil_done, t + 1)
                if not (isinstance(t, int) and t < 2):
                    dve.wait_ge(hid_T, t - 1)
                nc.vector.tensor_tensor(hid[:, i % 2, 0:H], pH[i % 2][:, 512:512 + H], sil[:, i % 2, 0:H],
                                        ALU.mult).then_inc(hid_ready, 1)

            def tile_dve(t, i):
                if known(t):
                    if t == NEWTON_AT:
                        newton(G - 1, 1)
                    if t == COPY_AT:
                        copy_xn2T(G - 1, pPost)
                    if t == PICK_AT:
                        pick(PAIRS - 1, last=True)
                    if t == PLACE_AT:
                        place(PAIRS - 1, pRank_last, pTot_last)
                    if t == PLAN_AT:
                        dve.wait_ge(slots_ready, PAIRS)
                        plan_tiles(FIRST, TILES - FIRST, True)
                if not known(t) or t + 2 < TILES:
                    copy_xt(t + 2, i + 2)
                if not known(t) or t > 0:
                    gated(t - 1, (i - 1) % RING)
                if not known(t) or t + 1 < TILES:
                    hidden(t + 1, i + 1)

            plan_tiles(0, FIRST, False)
            copy_aggT(G - 1)
            copy_xn2T(G - 2)
            copy_xt(0, 0)
            add_x(G - 1)
            moments(G - 1, 1)
            dve.wait_ge(logits_mm, G - 1)
            nc.vector.tensor_copy(lg[:, 0, 0:TG], pLogits[:, 0:TG]).then_inc(logits_copied, 1)
            copy_xt(1, 1)
            hidden(0, 0)
            for t in range(PEEL):
                tile_dve(t, t)
            with dve.Fori(PEEL, TILES - RING, RING) as t:
                for i in range(RING):
                    tile_dve(t + i, i)
            for t in range(TILES - RING, TILES):
                tile_dve(t, t)
            gated(TILES - 1, RING - 1)
            for n_ in range(NC):
                dve.wait_ge(res_loaded[n_], 16)
                for c_ in range(2):
                    v = xs[:, KC * n_:KC * n_ + KC]
                    if c_:
                        dve.wait_ge(res_added, 2 * n_ + 1)
                    nc.vector.tensor_tensor(v, v, res[:, KC * n_:KC * n_ + KC, c_], ALU.add).then_inc(res_added, 1)

        @block.tensor
        def _(pe):
            def aggregate(u, c):
                pe.wait_ge(e2_done, u + 1)
                for s in range(SRC):
                    k = SRC * c + s
                    last = nc.tensor.matmul(pAgg[:], msg[:, k], w[:, c % 2, s], start=(k == 0), stop=(k == K - 1))
                last.then_inc(agg_done, 1)

            def back(g):
                pe.wait_ge(aggT_copied, g + 1)
                if not (known(g) and g == 0):
                    pe.wait_ge(x2_done, g)
                for b in range(TG):
                    last = nc.tensor.transpose(pX[:, b], aggT[:, b * P:(b + 1) * P], ident[:])
                last.then_inc(x2_T, 1)

            def transpose_xn2(g, h, bank=pXn):
                pe.wait_ge(xn2_ready, g + 1)
                if not (known(g) and g == 0):
                    pe.wait_ge(xn2T_copied, g)
                for b in range(TG):
                    last = nc.tensor.transpose(bank[:, b], rows[:, 0, TG * h + b, 0:D], ident[:])
                last.then_inc(xn2_T, 1)

            def logits(g, h, pr, bank=pLogits):
                pe.wait_ge(xn2T_copied, g + 1)
                if not (known(pr) and pr == 0):
                    pe.wait_ge(slots_ready, pr)
                for b in range(TG):
                    last = nc.tensor.matmul(bank[:, TG * h + b], xn2T[:, b * P:(b + 1) * P], rwT[:], start=True, stop=True)
                last.then_inc(logits_mm, 1)

            def rank(pr, pRank=pRank, pTot=pTot):
                pe.wait_ge(picked, 2 * pr + 2)
                nc.tensor.matmul(pRank, upper[:], chosen[:], start=True, stop=False, skip_group_check=True)
                for b in range(T2 - 1):
                    nc.tensor.matmul(pRank[:, b + 1:], ones[:], chosen[:, b:b + 1].to_broadcast([P, T2 - 1 - b, E]),
                                     start=False, stop=b == T2 - 2, skip_group_check=True)
                for b in range(T2):
                    last = nc.tensor.matmul(pTot, ones[:], chosen[:, b], start=b == 0, stop=b == T2 - 1,
                                            skip_group_check=True)
                last.then_inc(rank_mm, 1)

            def messages(n):
                if n >= 4:
                    pe.wait_ge(msg_ready, TG * (n - 3))
                for b in range(TG):
                    last = nc.tensor.matmul(pP[n % 4][:, b], xT[:, TG * n + b], wc[:], start=True, stop=True)
                last.then_inc(msg_mm, 1)

            def steps(pr, first=False):
                for j in range(PU):
                    u, c = PU * pr + j, j % C
                    if first and j == 1:
                        for n in range(4, K // TG):
                            messages(n)
                    if not first:
                        if j == 0:
                            back(2 * pr - 1)
                        if j == 1:
                            transpose_xn2(2 * pr - 2, 0)
                        if j == 2:
                            logits(2 * pr - 2, 0, pr - 1)
                        if j == 3:
                            transpose_xn2(2 * pr - 1, 1)
                        if j == 4:
                            logits(2 * pr - 1, 1, pr - 1)
                        if j == 5:
                            rank(pr - 1)
                    if j == 4:
                        back(2 * pr)
                    if first and j < C:
                        pe.wait_ge(msg_ready, SRC * (j + 1))
                    aggregate(u, c)

            pe.wait_ge(ops_ready, 1)
            pe.wait_ge(wg_loaded, 16)
            nc.tensor.matmul(pSm[:, 0:D], mean_op[:], wg[:], start=True, stop=True).then_inc(colmean_mm, 1)
            pe.wait_ge(ident_ready, 1)
            pe.wait_ge(x_loaded, 16)
            for n in range(K // TG):
                if n >= 4:
                    pe.wait_ge(xT_copied, n - 3)
                for b in range(TG):
                    last = nc.tensor.transpose(pP[n % 4][:, b], xs[:, TG * n + b], ident[:])
                last.then_inc(x_T, 1)
            pe.wait_ge(wc_ready, 1)
            pe.wait_ge(xT_copied, K // TG)
            for n in range(4):
                messages(n)
            steps(0, first=True)
            pe.wait_ge(rw_loaded, 16)
            pe.wait_ge(tables_ready, 1)
            with pe.Fori(1, PAIRS) as pr:
                steps(pr)
            def turn(t, i):
                if known(t):
                    pe.wait_ge(xt_loaded[i % RING], 16 * (t // RING + 1))
                else:
                    pe.wait_ge(xt_loaded[i % RING], PER * (t - i % RING) + 16)
                if known(t) and t == 1:
                    pe.wait_ge(xtT_copied, 1)
                nc.tensor.transpose(pXT, xt[:, i % RING, 0:D], ident[:]).then_inc(xt_T, 1)

            def expert(t):
                return pe.value_load(tabi[0:1, 1, bass.ds(t, 1)], min_val=0, max_val=E - 1)

            def up(t, i, e):
                pe.wait_ge(xtT_copied, t + 1)
                nc.tensor.matmul(pH[i % 2][:, 0:H], xtT[:, i % 2], w1T[:, bass.ds(e * H, H)], start=True, stop=True)
                nc.tensor.matmul(pH[i % 2][:, 512:512 + H], xtT[:, i % 2], w3T[:, bass.ds(e * H, H)], start=True,
                                 stop=True).then_inc(h_mm, 1)

            def turn_hidden(t, i):
                pe.wait_ge(hid_ready, t + 1)
                if not isinstance(t, int) or t > 0:
                    pe.wait_ge(hidT_copied, t)
                for m in range(HT):
                    n = P if m < HT - 1 else HL
                    last = nc.tensor.transpose(pHT[0:n, m], hid[:, i % 2, m * P:m * P + n], ident[:])
                last.then_inc(hid_T, 1)

            def down(t, i, e):
                if known(t) and t == TILES - 1:
                    pe.wait_ge(hidT_copied, t + 1)
                if not known(t) or t > 0:
                    pe.wait_ge(y_out, t)
                for m in range(HT):
                    n = P if m < HT - 1 else HL
                    last = nc.tensor.matmul(pY, hidT[0:n, i % 2, m], w2T[0:n, bass.ds(e * (HT * D) + m * D, D)],
                                            start=m == 0, stop=m == HT - 1)
                last.then_inc(y_mm, 1)

            def tile_pe(t, i, experts):
                if known(t):
                    if t == XN_AT:
                        pe.wait_ge(x2_done, G)
                        transpose_xn2(G - 1, 1, pX)
                    if t == LOGITS_AT:
                        logits(G - 1, 0, PAIRS - 1, pLogits_last)
                    if t == RANK_AT:
                        rank(PAIRS - 1, pRank_last, pTot_last)
                if not known(t) or t + 1 < TILES:
                    experts.append(expert(t + 1))
                    up(t + 1, i + 1, experts[i + 1])
                if not known(t) or t + 2 < TILES:
                    turn(t + 2, i + 2)
                turn_hidden(t, i)
                if not known(t) or t > 0:
                    down(t - 1, i + 1, experts[i - 1] if i > 0 else expert(t - 1))

            transpose_xn2(G - 2, 0)
            pe.wait_ge(aggT_copied, G)
            turn(0, 0)
            back(G - 1)
            logits(G - 2, 0, PAIRS - 1)
            turn(1, 1)
            for n in range(2 + HT):
                pe.wait_ge(w_loaded[n], 16)
            experts = [expert(0)]
            up(0, 0, experts[0])
            for t in range(PEEL):
                if t == 1:
                    pe.wait_ge(logits_copied, 1)
                tile_pe(t, t, experts)
            with pe.Fori(PEEL, TILES - RING, BODY) as t:
                experts = [expert(t)]
                for i in range(BODY):
                    tile_pe(t + i, i, experts)
            experts = [expert(TILES - RING)]
            for i in range(RING):
                tile_pe(TILES - RING + i, i, experts)
            down(TILES - 1, RING - 1, experts[RING - 1])



_INS = ['x', 'adj', 'L0_gnn_W', 'L0_gnn_B', 'L0_ffn_router_w', 'L0_ffn_w1', 'L0_ffn_w2', 'L0_ffn_w3']
_OUTS = [((4096, 128), 'float32')]


def kernel(**inputs):
    import numpy as _np
    import concourse.bacc as _bacc
    from concourse import mybir as _mybir
    from concourse.bass_utils import run_bass_kernel_spmd as _run

    laid = {name: _np.asarray(inputs[name]) for name in _INS}
    adj, w1, w2, w3 = laid['adj'], laid['L0_ffn_w1'], laid['L0_ffn_w2'], laid['L0_ffn_w3']
    n = adj.shape[0]
    e, h, d = w1.shape
    gw, c = TG * P, n // (SRC * P)
    laid['adj'] = adj.reshape(n // gw, gw, c, SRC, P).transpose(0, 2, 4, 3, 1).reshape(n // gw, c, P, SRC * gw)
    laid['L0_ffn_router_w'] = laid['L0_ffn_router_w'].T
    laid['L0_ffn_w1'], laid['L0_ffn_w3'] = w1.reshape(e * h, d).T, w3.reshape(e * h, d).T
    laid['L0_ffn_w2'] = w2.transpose(2, 0, 1)

    nc = _bacc.Bacc("TRN2", target_bir_lowering=False, num_devices=1)
    arrays, args = {}, []
    for name in _INS:
        a = _np.ascontiguousarray(laid[name])
        arrays[f"in_{name}_dram"] = a
        args.append(nc.dram_tensor(f"in_{name}_dram", a.shape, _mybir.dt.from_np(a.dtype), kind="ExternalInput").ap())
    for i, (shape, dtype) in enumerate(_OUTS):
        dt = _mybir.dt.from_np(_np.dtype(dtype))
        args.append(nc.dram_tensor(f"out_{i}_dram", shape, dt, kind="ExternalOutput").ap())
    gnn_moe_layer(nc, *args)
    r = _run(nc, [arrays], core_ids=[0])
    return r.results[0]["out_0_dram"]
```

```python
import concourse.bass as bass
from concourse import mybir
from contextlib import ExitStack

F32 = mybir.dt.float32
BF16 = mybir.dt.bfloat16
U32 = mybir.dt.uint32
I32 = mybir.dt.int32
ALU = mybir.AluOpType
ACT = mybir.ActivationFunctionType
AX_X = mybir.AxisListType.X
P = 128
LN_EPS = 1e-5
TINY = 2.0 ** -60
TG = 4
SRC = 8


def gnn_moe_layer(nc, x, adjT, gnn_w, gnn_b, router_wT, w1_t, w2_t, w3_t, out):
    N, D = x.shape
    K = N // P
    G = K // TG
    C = K // SRC
    GW = TG * P
    HALF = SRC // 2
    PIECES = 4
    U = G * C
    PAIRS = G // 2
    T2 = 2 * TG
    PU = 2 * C
    _, EH = w1_t.shape
    H, E, _ = w2_t.shape
    HT = -(-H // P)
    HC = -(-H // HT)
    HL = H - (HT - 1) * HC
    CAP = N + P
    TILES = 2 * N // P + E
    ROW = D + 2
    GB, IDB = D, D + 1
    RING = 8
    FIRST = 2 * N * (PAIRS - 1) // PAIRS // P - E
    OLD = FIRST + 2 * E
    OLD_K = T2 * (PAIRS - 1)
    PART_K = OLD_K // RING
    LAST_PARTS = 4
    LAST_K = T2 // LAST_PARTS
    assert FIRST % RING == 0 and OLD == TILES - 2 * RING and OLD_K % RING == 0
    PER = 16 // RING
    assert TILES % RING == 0 and EH == E * H

    slots = nc.dram_tensor("slots", [E * CAP + E * P, ROW], F32, kind="Internal").ap()
    results = nc.dram_tensor("results", [2 * N + 2 * E * P, D], F32, kind="Internal").ap()

    x_v = x.rearrange("(k p) d -> p k d", p=P)
    out_v = out.rearrange("(k p) d -> p k d", p=P)

    with ExitStack() as ctx:
        def sb(name, shape, dt=F32):
            return ctx.enter_context(nc.sbuf_tensor(name, shape, dt))

        def pb(name, shape, dt=F32):
            return ctx.enter_context(nc.psum_tensor(name, shape, dt))

        def sem(name):
            return ctx.enter_context(nc.semaphore(name))

        r = sb("r", [P, C, SRC, GW])
        w = sb("w", [P, 2, SRC, GW])
        xs = sb("xs", [P, K, D])
        msg = sb("msg", [P, K, D])
        w2T = sb("w2T", [P, E * HT * D])
        shared = sb("shared", [P, 2, K * D])
        ident = sb("ident", [P, P])
        wg = sb("wg", [P, D])
        wc = sb("wc", [P, D])
        bg = sb("bg", [P, D])
        mean_op = sb("mean_op", [P, P])
        st1 = sb("st1", [P, 4, K])
        bn1 = sb("bn1", [P, K, 6])
        mv1 = sb("mv1", [P, K, 2])
        epsT = sb("epsT", [P, 2])
        bm2 = sb("bm2", [P, 1])
        upper = sb("upper", [P, P], BF16)
        ones = sb("ones", [P, P], BF16)
        rev = sb("rev", [P, E])
        ids = sb("ids", [P, K, 2], U32)
        rows = sb("rows", [P, 2, T2, ROW])
        pad = sb("pad", [P, E, ROW])
        pad_at = sb("pad_at", [1, E], I32)
        rwT = sb("rwT", [P, E])
        bnst = sb("bnst", [P, TG, 6])
        mv = sb("mv", [P, 2, TG, 2])
        st2 = sb("st2", [P, 2, 4, TG])
        lg = sb("lg", [P, 8, T2, E])
        chosen = sb("chosen", [P, T2, E], BF16)
        sm = sb("sm", [P, 10, T2])
        soft = sb("soft", [P, T2 * E + T2])
        softe = sb("softe", [P, T2 * E + T2])
        base = sb("base", [P, E])
        slot_at = sb("slot_at", [P, T2, 2], U32)
        tau = sb("tau", [1, TILES])
        nt = sb("nt", [1, 9, E])
        bounds = sb("bounds", [1, 3, 2 * E])
        nti = sb("nti", [1, 2, E], I32)
        tabi = sb("tabi", [1, 2, TILES + 2 * RING], I32)

        xT = shared[:, 0].rearrange("p (k d) -> p k d", d=D)
        w1T, w3T = shared[:, 0, 0:E * H], shared[:, 1, 0:E * H]
        aggT, xn2T = shared[:, 1, K * D - 2 * GW:K * D - GW], shared[:, 1, K * D - GW:]
        tab = shared[0:1, 0, E * H:E * H + TILES * E].rearrange("p (t e) -> p t e", e=E)
        tabf = shared[0:1, 0, E * H + TILES * E:E * H + TILES * (E + 3)].rearrange("p (a t) -> p a t", a=3)
        REST = TILES - FIRST
        at = E * H + TILES * (E + 3)
        tab2 = shared[0:1, 0, at:at + REST * 2 * E].rearrange("p (t e) -> p t e", e=2 * E)
        assert at + REST * 2 * E <= K * D and REST * 2 <= TILES
        yf = r[:].rearrange("p a s n -> p (a s n)")
        xt = yf[:, 0:RING * ROW].rearrange("p (i n) -> p i n", n=ROW)
        at = RING * ROW
        xtT = yf[:, at:at + 2 * P].rearrange("p (i n) -> p i n", n=P)
        at += 2 * P
        sil = yf[0:HC, at:at + 2 * HT * P].rearrange("p (i n) -> p i n", n=HT * P)
        at += 2 * HT * P
        hidT = yf[0:HC, at:at + 2 * HT * P].rearrange("p (i n) -> p i n", n=HT * P)
        at += 2 * HT * P
        W_RING = 4
        w13 = yf[:, at:at + W_RING * 2 * HT * HC].rearrange("p (i a h) -> p i a h", a=2, h=HT * HC)
        at += W_RING * 2 * HT * HC
        w2e = yf[:, at:at + 2 * HT * D].rearrange("p (i n) -> p i n", n=HT * D)
        at += 2 * HT * D
        assert at + RING * D <= 2 * SRC * GW
        yo = yf[:, at:at + RING * D].rearrange("p (i n) -> p i n", n=D)
        res = w[:].rearrange("p a s n -> p (a s n)").rearrange("p (k c d) -> p k c d", c=2, d=D)

        pH_ = pb("pH_", [P, 2, 2, GW])
        pAgg = pb("pAgg", [P, GW])
        pX = pb("pX", [P, TG, P])
        pXn = pb("pXn", [P, TG, P])
        pSm = pb("pSm", [P, GW])
        pLogits = pSm[:, 0:T2 * E].rearrange("p (b e) -> p b e", e=E)
        pRank = pSm[:, 128:128 + T2 * E].rearrange("p (b e) -> p b e", e=E)
        pTot = pSm[:, 256:256 + E]
        pPost = pX[:].rearrange("p b d -> p (b d)")
        pLogits_last = pPost[:, 0:TG * E].rearrange("p (b e) -> p b e", e=E)
        pRank_last = pPost[:, 128:128 + T2 * E].rearrange("p (b e) -> p b e", e=E)
        pTot_last = pPost[:, 256:256 + E]
        pP = [pH_[:, n // 2, n % 2].rearrange("p (b d) -> p b d", d=D) for n in range(4)]
        pH = [pH_[:, 0].rearrange("p s n -> p (s n)"), pH_[:, 1].rearrange("p s n -> p (s n)")]
        pXT = pAgg[:, 0:P]
        pY = pSm[:, 0:D]

        piece_loaded = [[sem(f"piece_loaded{c}_{q}") for q in range(PIECES - 1)] for c in range(2)]
        last_half = sem("last_half")
        r_loaded = [sem(f"r_loaded{c}") for c in range(C)]
        x_loaded, wg_loaded, bg_loaded, rw_loaded = sem("x_loaded"), sem("wg_loaded"), sem("bg_loaded"), sem("rw_loaded")
        w_loaded = [sem(f"w_loaded{n}") for n in range(2 + HT)]
        id0, ident_ready, consts_ready, ops_ready = sem("id0"), sem("ident_ready"), sem("consts_ready"), sem("ops_ready")
        masked, ln_done, e1_done, q_done, e2_done, agg_done = (sem("masked"), sem("ln_done"), sem("e1_done"),
                                                             sem("q_done"), sem("e2_done"), sem("agg_done"))
        colmean_mm, wc_ready = sem("colmean_mm"), sem("wc_ready")
        x_T, xT_copied, msg_mm, msg_ready = sem("x_T"), sem("xT_copied"), sem("msg_mm"), sem("msg_ready")
        bn1_done, var1_ready, ln1_act, newton1 = sem("bn1_done"), sem("var1_ready"), sem("ln1_act"), sem("newton1")
        aggT_copied, x2_T, x2_done = sem("aggT_copied"), sem("x2_T"), sem("x2_done")
        bn2_done, var2_ready, ln2_act, newton2, rstd2_ready = (sem("bn2_done"), sem("var2_ready"), sem("ln2_act"),
                                                               sem("newton2"), sem("rstd2_ready"))
        centred2, xn2_ready, xn2_copied, ids_placed = sem("centred2"), sem("xn2_ready"), sem("xn2_copied"), sem("ids_placed")
        xn2_T, xn2T_copied, logits_mm = sem("xn2_T"), sem("xn2T_copied"), sem("logits_mm")
        route = sem("route")
        soft_in, soft_done, picked, rank_mm, slots_ready = (sem("soft_in"), sem("soft_done"), sem("picked"),
                                                            sem("rank_mm"), sem("slots_ready"))
        tables_ready, pad_zeroed, pad_ids = sem("tables_ready"), sem("pad_zeroed"), sem("pad_ids")
        scattered, padded, dummies_stored = sem("scattered"), sem("padded"), sem("dummies_stored")
        plan, plan1_ready, plan2_ready, logits_copied = sem("plan"), sem("plan1_ready"), sem("plan2_ready"), sem("logits_copied")
        xt_loaded = [sem(f"xt_loaded{i}") for i in range(RING)]
        yt_stored = [sem(f"yt_stored{i}") for i in range(RING)]
        xt_T, xtT_copied, h_mm, sil_done, hid_ready, w13_copied, w2_copied, y_mm, y_out = (
            sem("xt_T"), sem("xtT_copied"), sem("h_mm"), sem("sil_done"), sem("hid_ready"), sem("w13_copied"),
            sem("w2_copied"), sem("y_mm"), sem("y_out"))
        res_loaded = [sem(f"res_loaded{n}") for n in range(RING + LAST_PARTS)]
        res_added, out_stored = sem("res_added"), sem("out_stored")
        END, SKIP2, HOP = range(3)
        padding_at = sem("padding_at")
        padding_zeroed, w2_zeroed = sem("padding_zeroed"), sem("w2_zeroed")
        stood = sem("stood")
        parts = [(PART_K * n, PART_K * (n + 1)) for n in range(RING)]
        parts += [(OLD_K + LAST_K * n, OLD_K + LAST_K * (n + 1)) for n in range(LAST_PARTS)]
        NEWTON_AT, XN_AT, COPY_AT, LOGITS_AT, PICK_AT, RANK_AT, PLACE_AT, PLAN_AT = 0, 2, 3, 4, 5, 8, 9, 13
        SCATTER_AT = PLACE_AT + 3
        PEEL = 3 * RING
        PEEL2 = RING * (-(-(SCATTER_AT + 2 * T2) // RING))
        assert PLAN_AT + 6 < PEEL and PEEL2 <= FIRST
        STORE = 16 * 2 * T2

        def known(t):
            return isinstance(t, int)

        def tiles_of(g):
            return slice(TG * g, TG * g + TG) if known(g) else bass.ds(TG * g, TG)

        block = ctx.enter_context(nc.Block())

        def load_at(sp, t, i):
            at = sp.value_load(tabi[0:1, 0, bass.ds(t, 1)], min_val=0, max_val=E * CAP + (E - 1) * P)
            sp.dma_start(xt[:, i], slots[bass.ds(at, P), :]).then_inc(xt_loaded[i], 16)

        def reload_ring(sp, t):
            for i in range(RING):
                sp.wait_ge(yt_stored[i], PER * t)
                sp.sem_inc(stood, 1)
                load_at(sp, t + i, i)

        @block.sync
        def _(sp):
            def load(g, c):
                sp.dma_start(r[:, c].rearrange("p s n -> p (s n)"), adjT[g, c]).then_inc(r_loaded[c], 16)

            for c in range(2):
                for q in range(PIECES):
                    sp.dma_start(r[:, c, SRC // PIECES * q:SRC // PIECES * (q + 1)].rearrange("p s n -> p (s n)"),
                                 adjT[0, c, :, SRC * GW // PIECES * q:SRC * GW // PIECES * (q + 1)]).then_inc(
                                     r_loaded[c] if q == PIECES - 1 else piece_loaded[c][q], 16)
                if c == 0:
                    sp.dma_start(wg[:], gnn_w).then_inc(wg_loaded, 16)
            sp.dma_start(xs[:], x_v).then_inc(x_loaded, 16)
            sp.dma_start(bg[:], gnn_b.rearrange("(a d) -> a d", a=1).to_broadcast([P, D])).then_inc(bg_loaded, 16)
            for c in range(2, C):
                load(0, c)
            sp.dma_start(rwT[:], router_wT).then_inc(rw_loaded, 16)
            for c in range(C):
                sp.wait_ge(e2_done, c + 1)
                load(1, c)
            sp.wait_ge(msg_ready, K)
            sp.dma_start(w1T, w1_t).then_inc(w_loaded[0], 16)
            sp.dma_start(w3T, w3_t).then_inc(w_loaded[1], 16)
            sp.wait_ge(w2_zeroed, 1)
            w2v = w2T[:].rearrange("p (e m d) -> p e m d", m=HT, d=D)
            for m in range(HT):
                n = HC if m < HT - 1 else HL
                sp.dma_start(w2v[0:n, :, m], w2_t[m * HC:m * HC + n]).then_inc(w_loaded[2 + m], 16)
            with sp.Fori(2, G) as g:
                for c in range(C):
                    sp.wait_ge(e2_done, C * g + c - C + 1)
                    load(g, c)

            sp.wait_ge(plan1_ready, 1)
            sp.wait_ge(scattered, STORE * (PAIRS - 1))
            sp.wait_ge(e2_done, U - 2)
            for i in range(RING):
                load_at(sp, i, i)
            with sp.Fori(RING, FIRST - RING, RING) as t:
                reload_ring(sp, t)
            sp.wait_ge(padding_at, 1)
            sp.wait_ge(pad_ids, 2)
            for i in range(RING):
                sp.wait_ge(yt_stored[i], PER * (FIRST - RING))
                load_at(sp, FIRST - RING + i, i)
                for e in range(i, E, RING):
                    at = sp.value_load(pad_at[0:1, e:e + 1], min_val=0, max_val=E * CAP - P)
                    sp.dma_start(slots[bass.ds(at, P), :], pad[:, e]).then_inc(padded, 16)
            sp.wait_ge(plan2_ready, 1)
            sp.wait_ge(dummies_stored, 16)
            sp.wait_ge(padded, 16 * E)
            sp.wait_ge(scattered, STORE * PAIRS)
            with sp.Fori(FIRST, TILES - RING, RING) as t:
                reload_ring(sp, t)
            rv = results[0:2 * N].rearrange("(k p c) d -> p k c d", p=P, c=2)

            def load_results(n):
                a, b = parts[n]
                sp.dma_start(res[:, a:b], rv[:, a:b]).then_inc(res_loaded[n], 16)

            def store_out(a, b, n):
                sp.wait_ge(res_added, n)
                sp.dma_start(out_v[:, a:b], xs[:, a:b]).then_inc(out_stored, 16)

            for i in range(RING):
                load_results(i)
                sp.wait_ge(yt_stored[i], PER * (TILES - RING))
                sp.sem_inc(stood, 1)
                load_at(sp, TILES - RING + i, i)
            for n in range(1, RING, 2):
                store_out(parts[n - 1][0], parts[n][1], 2 * n + 2)
            for i in range(RING):
                sp.wait_ge(yt_stored[i], PER * TILES)
            for n in range(RING, RING + LAST_PARTS):
                load_results(n)
            for n in range(RING, RING + LAST_PARTS):
                store_out(*parts[n], 2 * n + 2)
            sp.wait_ge(out_stored, 16 * (RING // 2 + LAST_PARTS))

        @block.gpsimd
        def _(pool):
            nc.gpsimd.memset(epsT[:, 0:1], TINY)
            nc.gpsimd.memset(bm2[:], -2.0)
            nc.gpsimd.memset(epsT[:, 1:2], LN_EPS).then_inc(consts_ready, 1)
            nc.gpsimd.memset(ident[:], 0.0).then_inc(id0, 1)
            pool.wait_ge(id0, 1)
            nc.gpsimd.affine_select(out=ident[:], in_=ident[:], compare_op=ALU.not_equal, fill=1.0, base=0,
                                    pattern=[[-1, P]], channel_multiplier=1).then_inc(ident_ready, 1)
            nc.gpsimd.memset(mean_op[:], 1.0 / D).then_inc(ops_ready, 1)
            nc.gpsimd.memset(ones[:], 1.0).then_inc(id0, 1)
            pool.wait_ge(id0, 2)
            nc.gpsimd.affine_select(out=upper[:], in_=ones[:], compare_op=ALU.is_gt, fill=0.0, base=0,
                                    pattern=[[1, P]], channel_multiplier=-1)
            nc.gpsimd.iota(ids[:], [[2 * P, K], [1, 2]], base=0, channel_multiplier=2)
            nc.gpsimd.iota(rev[:], [[-1, E]], base=E, channel_multiplier=0, allow_small_or_imprecise_dtypes=True)
            nc.gpsimd.iota(base[:], [[CAP, E]], base=0, channel_multiplier=0, allow_small_or_imprecise_dtypes=True)
            nc.gpsimd.memset(bounds[:, HOP, :], 1.0).then_inc(id0, 1)
            pool.wait_ge(id0, 3)
            nc.gpsimd.memset(bounds[:, HOP, E - 1:E], 1.0 - E)
            nc.gpsimd.iota(tau[:], [[1, TILES]], base=0, channel_multiplier=0,
                           allow_small_or_imprecise_dtypes=True).then_inc(tables_ready, 1)
            pool.wait_ge(tables_ready, 1)
            nc.gpsimd.memset(pad[:], 0.0).then_inc(pad_zeroed, 1)
            pool.wait_ge(pad_zeroed, 1)
            nc.gpsimd.memset(w2T[HL // 32 * 32:], 0.0).then_inc(w2_zeroed, 1)
            pool.wait_ge(w2_zeroed, 1)
            nc.gpsimd.iota(pad[:, :, IDB:IDB + 1].bitcast(U32), [[P, E], [0, 1]], base=2 * N + E * P,
                           channel_multiplier=1).then_inc(pad_ids, 1)
            pool.wait_ge(pad_ids, 1)
            pool.dma_start(slots[E * CAP:E * CAP + E * P].rearrange("(e p) n -> p e n", p=P),
                           pad[:]).then_inc(dummies_stored, 16)
            pool.wait_ge(dummies_stored, 16)
            nc.gpsimd.iota(pad[:, :, IDB:IDB + 1].bitcast(U32), [[P, E], [0, 1]], base=2 * N,
                           channel_multiplier=1).then_inc(pad_ids, 1)

            def normalise(g, h, pr):
                if h == 0 and not (known(pr) and pr == 0):
                    pool.wait_ge(scattered, STORE * pr)
                pool.wait_ge(rstd2_ready, g + 1)
                a, b = rows[:, 0, TG * h:TG * h + TG, 0:D], rows[:, 1, TG * h:TG * h + TG, 0:D]
                nc.gpsimd.tensor_tensor(b, xs[:, tiles_of(g)], mv[:, h, :, 0:1].to_broadcast([P, TG, D]),
                                        ALU.subtract).then_inc(centred2, 1)
                pool.wait_ge(centred2, g + 1)
                nc.gpsimd.tensor_tensor(a, b, st2[:, h, 2].unsqueeze(2).to_broadcast([P, TG, D]),
                                        ALU.mult).then_inc(xn2_ready, 1)
                pool.wait_ge(xn2_ready, g + 1)
                pool.sem_inc(stood, 1)
                nc.gpsimd.tensor_copy(b, a).then_inc(xn2_copied, 1)

            def scatter_tile(b, ch):
                pool.indirect_dma_start(slots, bass.IndirectOffsetOnAxis(slot_at[:, b, ch:ch + 1], 0),
                                        rows[:, ch, b], None).then_inc(scattered, 16)

            def number(pr):
                for ch in range(2):
                    nc.gpsimd.tensor_copy(rows[:, ch, :, IDB:IDB + 1].bitcast(U32),
                                          ids[:, slice(T2 * pr, T2 * pr + T2) if known(pr) else bass.ds(T2 * pr, T2),
                                              ch:ch + 1]).then_inc(ids_placed, 1)
                pool.wait_ge(ids_placed, 2 * pr + 2)
                pool.wait_ge(xn2_copied, 2 * pr + 2)
                pool.wait_ge(slots_ready, pr + 1)
                pool.sem_inc(stood, 1)
            normalise(0, 0, 0)
            with pool.Fori(1, PAIRS) as pr:
                normalise(2 * pr - 1, 1, pr - 1)
                number(pr - 1)
                for b in range(T2):
                    for ch in range(2):
                        scatter_tile(b, ch)
                normalise(2 * pr, 0, pr)

            def store_tile(t, i):
                pool.wait_ge(y_out, t + 1)
                pool.sem_inc(stood, 1)
                pool.indirect_dma_start(results, bass.IndirectOffsetOnAxis(xt[:, i, IDB:IDB + 1].bitcast(U32), 0),
                                        yo[:, i], None).then_inc(yt_stored[i], 16)

            normalise(G - 1, 1, PAIRS - 1)
            for t in range(PEEL2):
                store_tile(t, t % RING)
                n = t - SCATTER_AT
                if n == 0:
                    number(PAIRS - 1)
                if 0 <= n < 2 * T2:
                    scatter_tile(n // 2, n % 2)
            with pool.Fori(PEEL2, TILES, RING) as t:
                for i in range(RING):
                    store_tile(t + i, i)

        @block.scalar
        def _(act):
            def ln(u, c):
                act.wait_ge(masked, u - 1 + 2 * PIECES)
                nc.scalar.activation(r[:, c], r[:, c], ACT.Ln, bias=epsT[:, 0:1]).then_inc(ln_done, 1)

            def ln_pieces(u):
                for q in range(PIECES):
                    act.wait_ge(masked, PIECES * u + q + 1)
                    v = r[:, u, SRC // PIECES * q:SRC // PIECES * (q + 1)]
                    nc.scalar.activation(v, v, ACT.Ln, bias=epsT[:, 0:1]).then_inc(ln_done, 1)

            def inverse(u, c):
                act.wait_ge(ln_done, PIECES * (u + 1) if known(u) and u < 2 else u - 1 + 2 * PIECES)
                nc.scalar.activation(r[:, c], r[:, c], ACT.Exp, scale=-1.0).then_inc(e1_done, 1)

            def weigh(u, c):
                act.wait_ge(q_done, u + 1)
                if not (known(u) and u < 2):
                    act.wait_ge(agg_done, u - 1)
                if known(u) and u >= U - 2:
                    nc.scalar.activation(w[:, c % 2, 0:HALF], r[:, c, 0:HALF], ACT.Exp, scale=-2.0,
                                         bias=bm2[:, 0:1]).then_inc(last_half, 1)
                    nc.scalar.activation(w[:, c % 2, HALF:], r[:, c, HALF:], ACT.Exp, scale=-2.0,
                                         bias=bm2[:, 0:1]).then_inc(e2_done, 1)
                else:
                    nc.scalar.activation(w[:, c % 2], r[:, c], ACT.Exp, scale=-2.0, bias=bm2[:, 0:1]).then_inc(e2_done, 1)

            def rstd2(g, h):
                act.wait_ge(var2_ready, g + 1)
                if not (known(g) and g < 2):
                    act.wait_ge(rstd2_ready, g - 1)
                nc.scalar.activation(st2[:, h, 0], mv[:, h, :, 1], ACT.Ln, bias=epsT[:, 1:2]).then_inc(ln2_act, 1)
                act.wait_ge(ln2_act, 2 * g + 1)
                nc.scalar.activation(st2[:, h, 1], st2[:, h, 0], ACT.Exp, scale=-0.5).then_inc(ln2_act, 1)

            def softmax_exp(pr):
                act.wait_ge(soft_in, pr + 1)
                nc.scalar.activation(softe[:], soft[:], ACT.Exp).then_inc(soft_done, 1)

            def steps(pr, first=False, last=False):
                for j in range(PU):
                    u, c = PU * pr + j, j % C
                    ahead = not (last and j == PU - 1)
                    if first and j == 0:
                        ln_pieces(1)
                    elif ahead:
                        ln(u + 1, (c + 1) % C)
                    if j == 2 and not first:
                        rstd2(2 * pr - 1, 1)
                    if j == 5 and not first:
                        softmax_exp(pr - 1)
                    if j == 7:
                        rstd2(2 * pr, 0)
                    if first and j == 1:
                        act.wait_ge(var1_ready, 1)
                        nc.scalar.activation(st1[:, 0], mv1[:, :, 1], ACT.Ln, bias=epsT[:, 1:2]).then_inc(ln1_act, 1)
                        act.wait_ge(ln1_act, 1)
                        nc.scalar.activation(st1[:, 1], st1[:, 0], ACT.Exp, scale=-0.5).then_inc(ln1_act, 1)
                    if ahead:
                        inverse(u + 1, (c + 1) % C)
                    weigh(u, c)
                    if first and j == 0:
                        for n in range(K // TG):
                            act.wait_ge(x_T, n + 1)
                            nc.scalar.activation(xT[:, TG * n:TG * n + TG], pP[n % 4], ACT.Copy).then_inc(xT_copied, 1)

            act.wait_ge(consts_ready, 1)
            nc.scalar.preload_act_table_set("natural_log_exp_and_others")
            ln_pieces(0)
            inverse(0, 0)
            steps(0, first=True)
            with act.Fori(1, PAIRS - 1) as pr:
                steps(pr)
            steps(PAIRS - 1, last=True)

            def silu(t, i):
                act.wait_ge(h_mm, t + 1)
                if not (known(t) and t < 2):
                    act.wait_ge(hid_ready, t - 1)
                nc.scalar.activation(sil[:, i % 2], pH[i % 2][0:HC, 0:HT * P], ACT.Silu).then_inc(sil_done, 1)

            def copy_xt(t, i):
                act.wait_ge(xt_T, t + 1)
                nc.scalar.activation(xtT[:, i % 2], pXT, ACT.Copy).then_inc(xtT_copied, 1)

            def gated(t, i):
                act.wait_ge(y_mm, t + 1)
                if not (known(t) and t < RING):
                    act.wait_ge(yt_stored[i % RING], 16 * (t // RING) if known(t) else PER * (t - i % RING))
                nc.scalar.activation(yo[:, i % RING], pY, ACT.Copy, scale=xt[:, i % RING, GB:GB + 1]).then_inc(y_out, 1)

            def tile_act(t, i):
                if known(t) and t == RANK_AT:
                    softmax_exp(PAIRS - 1)
                if not known(t) or t + 2 < TILES:
                    copy_xt(t + 2, i + 2)
                if not known(t) or t + 1 < TILES:
                    silu(t + 1, i + 1)
                if not known(t) or t > 0:
                    gated(t - 1, (i - 1) % RING)

            copy_xt(0, 0)
            rstd2(G - 1, 1)
            copy_xt(1, 1)
            silu(0, 0)
            for t in range(PEEL):
                tile_act(t, t)
            with act.Fori(PEEL, TILES - RING, RING) as t:
                for i in range(RING):
                    tile_act(t + i, i)
            for t in range(TILES - RING, TILES):
                tile_act(t, t)
            gated(TILES - 1, RING - 1)

        @block.vector
        def _(dve):
            def masking(v):
                nc.vector.scalar_tensor_tensor(out=v, in0=v, scalar=1.0, in1=v, op0=ALU.is_lt,
                                               op1=ALU.mult).then_inc(masked, 1)

            def mask(g, c):
                dve.wait_ge(r_loaded[c], 16 * (g + 1))
                masking(r[:, c])

            def exponent(u, c):
                dve.wait_ge(e1_done, u + 1)
                nc.vector.scalar_tensor_tensor(out=r[:, c], in0=r[:, c], scalar=2.0, in1=r[:, c], op0=ALU.subtract,
                                               op1=ALU.mult).then_inc(q_done, 1)

            def copy_aggT(g):
                dve.wait_ge(agg_done, C * (g + 1))
                if not (known(g) and g == 0):
                    dve.wait_ge(x2_T, g)
                nc.vector.tensor_copy(aggT, pAgg[:]).then_inc(aggT_copied, 1)

            def add_x(g):
                dve.wait_ge(x2_T, g + 1)
                nc.vector.tensor_tensor(xs[:, tiles_of(g)], pX[:], xs[:, tiles_of(g)], ALU.add).then_inc(x2_done, 1)

            def moments(g, h):
                dve.wait_ge(x2_done, g + 1)
                if not (known(g) and g < 2):
                    dve.wait_ge(xn2_ready, g - 1)
                dve.sem_inc(stood, 1)
                for b in range(TG):
                    v = xs[:, TG * g + b] if known(g) else xs[:, bass.ds(TG * g + b, 1)].rearrange("p a d -> p (a d)")
                    nc.vector.bn_stats(bnst[:, b], v).then_inc(bn2_done, 1)
                dve.wait_ge(bn2_done, TG * (g + 1))
                dve.sem_inc(stood, 1)
                for b in range(TG):
                    last = nc.vector.bn_aggr(mv[:, h, b], bnst[:, b])
                last.then_inc(var2_ready, 1)

            def newton(g, h):
                dve.wait_ge(ln2_act, 2 * g + 2)
                s = st2[:, h]
                nc.vector.tensor_scalar(s[:, 2], mv[:, h, :, 1], -0.5, -0.5 * LN_EPS, ALU.mult, ALU.add).then_inc(newton2, 1)
                nc.vector.tensor_tensor(s[:, 3], s[:, 1], s[:, 1], ALU.mult).then_inc(newton2, 1)
                dve.wait_ge(newton2, 3 * g + 2)
                nc.vector.tensor_tensor(s[:, 3], s[:, 3], s[:, 2], ALU.mult).then_inc(newton2, 1)
                dve.wait_ge(newton2, 3 * g + 3)
                nc.vector.scalar_tensor_tensor(out=s[:, 2], in0=s[:, 3], scalar=1.5, in1=s[:, 1], op0=ALU.add,
                                               op1=ALU.mult).then_inc(rstd2_ready, 1)

            def copy_xn2T(g, bank=None):
                dve.wait_ge(xn2_T, g + 1)
                if not (known(g) and g == 0):
                    dve.wait_ge(logits_mm, g)
                nc.vector.tensor_copy(xn2T, pXn[:].rearrange("p b d -> p (b d)") if bank is None else bank).then_inc(
                    xn2T_copied, 1)

            def bc(v):
                return v.unsqueeze(2).to_broadcast([P, T2, E])

            revb = rev[:].unsqueeze(1).to_broadcast([P, T2, E])
            PICK, PLACE, STEPS = 11, 19, 26

            class Steps:
                def __init__(self, pr, n):
                    self.pr, self.n = pr, n

                def __call__(self, ins):
                    ins.then_inc(route, 1)
                    self.n += 1

                def after(self):
                    dve.wait_ge(route, STEPS * self.pr + self.n)

            def pick_first(pr, last=False):
                dve.wait_ge(logits_mm, 2 * pr + 2)
                do = Steps(pr, 0)
                L, A, t0 = lg[:, 0], lg[:, 1], lg[:, 3]
                if last:
                    do(nc.vector.tensor_copy(L[:, TG:], pLogits_last))
                else:
                    do(nc.vector.tensor_copy(L, pLogits))
                do.after()
                top(do, 0, L, t0)
                do(nc.vector.tensor_tensor(A, t0, bc(sm[:, 2]), ALU.is_equal))

            def top(do, n, src, t0):
                do(nc.vector.reduce_max(sm[:, n], src, AX_X))
                do.after()
                do(nc.vector.tensor_tensor(t0, src, bc(sm[:, n]), ALU.is_equal))
                do.after()
                do(nc.vector.tensor_tensor(t0, t0, revb, ALU.mult))
                do.after()
                do(nc.vector.reduce_max(sm[:, 2], t0, AX_X))
                do.after()

            def pick_second(pr):
                do = Steps(pr, 6)
                L, A, B, t0, rest = lg[:, 0], lg[:, 1], lg[:, 2], lg[:, 3], lg[:, 5]
                do.after()
                do(nc.vector.scalar_tensor_tensor(out=rest, in0=A, scalar=-3.0e38, in1=L, op0=ALU.mult, op1=ALU.add))
                do.after()
                top(do, 1, rest, t0)
                nc.vector.tensor_tensor(B, t0, bc(sm[:, 2]), ALU.is_equal).then_inc(picked, 1)
                nc.vector.tensor_tensor(soft[:, 0:T2 * E].rearrange("p (b e) -> p b e", e=E), L, bc(sm[:, 0]), ALU.subtract)
                nc.vector.tensor_tensor(soft[:, T2 * E:], sm[:, 1], sm[:, 0], ALU.subtract).then_inc(soft_in, 1)
                dve.wait_ge(picked, 2 * pr + 1)
                nc.vector.tensor_tensor(chosen[:], A, B, ALU.add).then_inc(picked, 1)
                assert do.n == PICK, do.n

            def place(pr, pRank=pRank, pTot=pTot):
                do = Steps(pr, PICK)
                A, B, V, VA, VB = lg[:, 1], lg[:, 2], lg[:, 3], lg[:, 6], lg[:, 7]
                dve.wait_ge(rank_mm, pr + 1)
                do(nc.vector.tensor_tensor(V, pRank, base[:].unsqueeze(1).to_broadcast([P, T2, E]), ALU.add))
                do.after()
                do(nc.vector.tensor_tensor(VA, V, A, ALU.mult))
                do(nc.vector.tensor_tensor(VB, V, B, ALU.mult))
                do(nc.vector.tensor_tensor(base[:], pTot, base[:], ALU.add))
                do.after()
                do(nc.vector.reduce_sum(sm[:, 3], VA, AX_X))
                do(nc.vector.reduce_sum(sm[:, 4], VB, AX_X))
                do.after()
                do(nc.vector.tensor_copy(slot_at[:, :, 0], sm[:, 3]))
                do(nc.vector.tensor_copy(slot_at[:, :, 1], sm[:, 4]))
                assert do.n == PLACE, do.n

            def gates(pr):
                do = Steps(pr, PLACE)
                dve.wait_ge(soft_done, pr + 1)
                do(nc.vector.reduce_sum(sm[:, 5], softe[:, 0:T2 * E].rearrange("p (b e) -> p b e", e=E), AX_X))
                do.after()
                do(nc.vector.reciprocal(sm[:, 6], sm[:, 5]))
                do.after()
                do(nc.vector.tensor_tensor(sm[:, 7], softe[:, T2 * E:], sm[:, 6], ALU.mult))
                do.after()
                do(nc.vector.tensor_tensor(sm[:, 8], sm[:, 6], sm[:, 7], ALU.add))
                do.after()
                do(nc.vector.tensor_scalar(sm[:, 8], sm[:, 8], 1e-9, None, ALU.add))
                do.after()
                do(nc.vector.reciprocal(sm[:, 9], sm[:, 8]))
                do.after()
                do(nc.vector.tensor_tensor(rows[:, 0, :, GB], sm[:, 6], sm[:, 9], ALU.mult))
                nc.vector.tensor_tensor(rows[:, 1, :, GB], sm[:, 7], sm[:, 9], ALU.mult).then_inc(slots_ready, 1)
                assert do.n == STEPS, do.n

            def steps(pr, first=False, last=False):
                for j in range(PU):
                    u, c = PU * pr + j, j % C
                    exponent(u, c)
                    if first and j == 0:
                        dve.wait_ge(x_loaded, 16)
                        for k in range(K):
                            nc.vector.bn_stats(bn1[:, k], xs[:, k]).then_inc(bn1_done, 1)
                        mask(0, 2)
                        dve.wait_ge(bn1_done, K)
                        for k in range(K):
                            ins = nc.vector.bn_aggr(mv1[:, k], bn1[:, k])
                        ins.then_inc(var1_ready, 1)
                    if first and j == 1:
                        newton1_step()
                        messages(0)
                        mask(0, 3)
                    if j == 1 and not first:
                        add_x(2 * pr - 1)
                        moments(2 * pr - 1, 1)
                    if j == 6:
                        add_x(2 * pr)
                        moments(2 * pr, 0)
                    if not (last and j >= PU - 2) and not (first and j < 2):
                        mask(2 * pr + (j + 2) // C, (j + 2) % C)
                    if first and j == 2:
                        messages(1)
                    if first and j == 3:
                        for n in range(2, C):
                            messages(n)
                    if not first:
                        if j == 0:
                            copy_aggT(2 * pr - 1)
                        if j == 1:
                            copy_xn2T(2 * pr - 2)
                        if j == 2:
                            newton(2 * pr - 1, 1)
                        if j == 3:
                            copy_xn2T(2 * pr - 1)
                    if j == 4:
                        copy_aggT(2 * pr)
                    if not first:
                        if j == 4:
                            pick_first(pr - 1)
                            pick_second(pr - 1)
                        if j == 5:
                            place(pr - 1)
                            gates(pr - 1)
                    if j == 7:
                        newton(2 * pr, 0)

            def newton1_step():
                dve.wait_ge(ln1_act, 2)
                s = st1
                nc.vector.tensor_scalar(s[:, 2], mv1[:, :, 1], -0.5, -0.5 * LN_EPS, ALU.mult, ALU.add).then_inc(newton1, 1)
                nc.vector.tensor_tensor(s[:, 3], s[:, 1], s[:, 1], ALU.mult).then_inc(newton1, 1)
                dve.wait_ge(newton1, 2)
                nc.vector.tensor_tensor(s[:, 3], s[:, 3], s[:, 2], ALU.mult).then_inc(newton1, 1)
                dve.wait_ge(newton1, 3)
                nc.vector.scalar_tensor_tensor(out=s[:, 2], in0=s[:, 3], scalar=1.5, in1=s[:, 1], op0=ALU.add,
                                               op1=ALU.mult).then_inc(newton1, 1)

            def messages(c):
                if c == 0:
                    dve.wait_ge(newton1, 4)
                    dve.wait_ge(bg_loaded, 16)
                for k in range(SRC * c, SRC * c + SRC):
                    if k % TG == 0:
                        dve.wait_ge(msg_mm, k // TG + 1)
                    nc.vector.scalar_tensor_tensor(out=msg[:, k], in0=pP[k // TG % 4][:, k % TG], scalar=st1[:, 2, k:k + 1],
                                                   in1=bg[:], op0=ALU.mult, op1=ALU.add).then_inc(msg_ready, 1)

            for c in range(2):
                for q in range(PIECES):
                    dve.wait_ge(r_loaded[c] if q == PIECES - 1 else piece_loaded[c][q], 16)
                    masking(r[:, c, SRC // PIECES * q:SRC // PIECES * (q + 1)])
                if c == 0:
                    dve.wait_ge(colmean_mm, 1)
                    nc.vector.tensor_tensor(wc[:], wg[:], pSm[:, 0:D], ALU.subtract).then_inc(wc_ready, 1)
            steps(0, first=True)
            dve.wait_ge(tables_ready, 1)
            with dve.Fori(1, PAIRS - 1) as pr:
                steps(pr)
            steps(PAIRS - 1, last=True)
            class Links:
                n = 0

                def __call__(self, ins):
                    ins.then_inc(plan, 1)
                    self.n += 1
                    dve.wait_ge(plan, self.n)

            link = Links()
            CNT, NT, CUM, SKIP, DONE, SUM2, SUM4, SEEN, ALL = range(9)

            def slots_used():
                link(nc.vector.scalar_tensor_tensor(out=nt[:, CNT], in0=rev[0:1, :], scalar=float(CAP), in1=base[0:1, :],
                                                    op0=ALU.mult, op1=ALU.add))

            def tiles_of_slots(dst, up):
                link(nc.vector.tensor_scalar(nti[:, 0], nt[:, CNT], float((P - 1 if up else 0) - E * CAP), None, ALU.add))
                link(nc.vector.tensor_scalar(nti[:, 1], nti[:, 0], P.bit_length() - 1, None, ALU.logical_shift_right))
                link(nc.vector.tensor_copy(nt[:, dst], nti[:, 1]))

            def sum_tiles():
                for src, dst, n in ((NT, SUM2, 1), (SUM2, SUM4, 2), (SUM4, CUM, 4)):
                    link(nc.vector.tensor_copy(nt[:, dst, 0:n], nt[:, src, 0:n]))
                    link(nc.vector.tensor_tensor(nt[:, dst, n:], nt[:, src, n:], nt[:, src, 0:E - n], ALU.add))

            def first_slots(lo, n, tab, skip, ready):
                link(nc.vector.tensor_tensor(tab, tab, skip.unsqueeze(1).to_broadcast(list(tab.shape)), ALU.mult))
                link(nc.vector.reduce_sum(tabf[:, 1, 0:n], tab, AX_X))
                if lo:
                    link(nc.vector.scalar_tensor_tensor(out=tabf[:, 1, 0:n], in0=nt[:, DONE, 0:1].to_broadcast([1, n]),
                                                        scalar=float(P), in1=tabf[:, 1, 0:n], op0=ALU.mult, op1=ALU.add))
                link(nc.vector.scalar_tensor_tensor(out=tabf[:, 2, 0:n], in0=tau[:, 0:n], scalar=float(P),
                                                    in1=tabf[:, 1, 0:n], op0=ALU.mult, op1=ALU.add))
                nc.vector.tensor_copy(tabi[:, 0, lo:lo + n], tabf[:, 2, 0:n]).then_inc(ready, 1)

            def plan_first():
                slots_used()
                tiles_of_slots(NT, up=False)
                tiles_of_slots(SEEN, up=True)
                link(nc.vector.tensor_scalar(nt[:, SKIP], nt[:, NT], -float(P), float(CAP), ALU.mult, ALU.add))
                sum_tiles()
                t8 = tab[:, 0:FIRST]
                link(nc.vector.tensor_tensor(t8, tau[:, 0:FIRST].unsqueeze(2).to_broadcast([1, FIRST, E]),
                                             nt[:, CUM:CUM + 1].to_broadcast([1, FIRST, E]), ALU.is_ge))
                link(nc.vector.reduce_sum(tabf[:, 0, 0:FIRST], t8, AX_X))
                link(nc.vector.tensor_scalar(tabi[:, 1, 0:FIRST], tabf[:, 0, 0:FIRST], float(E - 1), None, ALU.min))
                first_slots(0, FIRST, t8, nt[:, SKIP], plan1_ready)

            def plan_second():
                link(nc.vector.tensor_scalar(nt[:, CNT], nt[:, CUM], float(FIRST), None, ALU.min))
                link(nc.vector.tensor_copy(nt[:, DONE, 0:1], nt[:, CNT, 0:1]))
                link(nc.vector.tensor_tensor(nt[:, DONE, 1:E], nt[:, CNT, 1:E], nt[:, CNT, 0:E - 1], ALU.subtract))
                link(nc.vector.tensor_tensor(nt[:, NT], nt[:, SEEN], nt[:, DONE], ALU.subtract))
                sum_tiles()
                link(nc.vector.tensor_copy(bounds[:, END, 0:E], nt[:, CUM]))
                link(nc.vector.tensor_tensor(nt[:, SKIP, 0:E - 1], nt[:, DONE, 1:E], nt[:, SEEN, 0:E - 1], ALU.subtract))
                link(nc.vector.tensor_tensor(nt[:, SKIP, E - 1:E], nt[:, SEEN, 0:1], nt[:, SEEN, E - 1:E], ALU.subtract))
                link(nc.vector.tensor_scalar(bounds[:, SKIP2, 0:E - 1], nt[:, SKIP, 0:E - 1], float(P), float(CAP),
                                             ALU.mult, ALU.add))
                link(nc.vector.tensor_scalar(bounds[:, SKIP2, E - 1:E], nt[:, SKIP, E - 1:E], float(P), -float((E - 1) * CAP),
                                             ALU.mult, ALU.add))

            def plan_third():
                nc.vector.tensor_copy(pad_at[:], base[0:1, :]).then_inc(padding_at, 1)
                slots_used()
                tiles_of_slots(ALL, up=True)
                link(nc.vector.tensor_tensor(nt[:, NT], nt[:, ALL], nt[:, SEEN], ALU.subtract))

            def bound_third():
                sum_tiles()
                link(nc.vector.tensor_tensor(bounds[:, END, E:], nt[:, CUM], bounds[:, END, E - 1:E].to_broadcast([1, E]),
                                             ALU.add))
                link(nc.vector.tensor_tensor(nt[:, SKIP, 0:E - 1], nt[:, SEEN, 1:E], nt[:, ALL, 0:E - 1], ALU.subtract))
                link(nc.vector.tensor_scalar(bounds[:, SKIP2, E:2 * E - 1], nt[:, SKIP, 0:E - 1], float(P), float(CAP),
                                             ALU.mult, ALU.add))
                link(nc.vector.tensor_scalar(bounds[:, SKIP2, 2 * E - 1:], nt[:, ALL, E - 1:E], -float(P), float(CAP),
                                             ALU.mult, ALU.add))

            both = tab[:].rearrange("p t e -> p (t e)")[:, 0:REST * 2 * E].rearrange("p (t e) -> p t e", e=2 * E)

            def experts_of_rest():
                link(nc.vector.tensor_tensor(both, tau[:, 0:REST].unsqueeze(2).to_broadcast([1, REST, 2 * E]),
                                             bounds[:, END:END + 1].to_broadcast([1, REST, 2 * E]), ALU.is_ge))
                link(nc.vector.tensor_tensor(tab2, both, bounds[:, HOP:HOP + 1].to_broadcast([1, REST, 2 * E]), ALU.mult))
                link(nc.vector.reduce_sum(tabf[:, 0, 0:REST], tab2, AX_X))
                link(nc.vector.tensor_scalar(tabi[:, 1, FIRST:TILES], tabf[:, 0, 0:REST], float(E - 1), None, ALU.min))

            def expert(t):
                return dve.value_load(tabi[0:1, 1, bass.ds(t, 1)], min_val=0, max_val=E - 1)

            def copy_w13(t, i, e):
                nc.vector.tensor_copy(w13[:, i % W_RING, :, 0:H], shared[:, :, bass.ds(e * H, H)]).then_inc(w13_copied, 1)

            def copy_w2(t, i, e):
                nc.vector.tensor_copy(w2e[0:HC, i % 2], w2T[0:HC, bass.ds(e * (HT * D), HT * D)]).then_inc(w2_copied, 1)

            def hidden(t, i):
                dve.wait_ge(sil_done, t + 1)
                if not (known(t) and t < 2):
                    dve.wait_ge(y_mm, t - 1)
                nc.vector.tensor_tensor(hidT[:, i % 2], pH[i % 2][0:HC, GW:GW + HT * P], sil[:, i % 2],
                                        ALU.mult).then_inc(hid_ready, 1)

            def add_results(n):
                a, b = parts[n]
                dve.wait_ge(res_loaded[n], 16)
                nc.vector.tensor_tensor(xs[:, a:b], xs[:, a:b], res[:, a:b, 0], ALU.add).then_inc(res_added, 1)
                dve.wait_ge(res_added, 2 * n + 1)
                nc.vector.tensor_tensor(xs[:, a:b], xs[:, a:b], res[:, a:b, 1], ALU.add).then_inc(res_added, 1)

            def tile_dve(t, i, experts):
                if known(t):
                    if t == NEWTON_AT:
                        newton(G - 1, 1)
                    if t == COPY_AT:
                        copy_xn2T(G - 1, pPost)
                    if t == PICK_AT:
                        pick_first(PAIRS - 1, last=True)
                    if t == PICK_AT + 2:
                        pick_second(PAIRS - 1)
                    if t == PLACE_AT:
                        place(PAIRS - 1, pRank_last, pTot_last)
                    if t == PLACE_AT + 2:
                        gates(PAIRS - 1)
                    if t == 1:
                        plan_second()
                    if t == PLAN_AT:
                        plan_third()
                    if t == PLAN_AT + 2:
                        bound_third()
                    if t == PLAN_AT + 4:
                        experts_of_rest()
                    if t == PLAN_AT + 6:
                        first_slots(FIRST, REST, both, bounds[:, SKIP2], plan2_ready)
                if not known(t) or t + 3 < TILES:
                    experts.append(expert(t + 3))
                    copy_w13(t + 3, i + 3, experts[i + 2])
                if not known(t) or t + 1 < TILES:
                    hidden(t + 1, i + 1)
                    copy_w2(t + 1, i + 1, experts[i])

            plan_first()
            dve.wait_ge(e2_done, U - 2)
            for n in range(2 + HT):
                dve.wait_ge(w_loaded[n], 16)
            nc.vector.memset(w13[:, :, :, H:], 0.0).then_inc(padding_zeroed, 1)
            dve.wait_ge(plan1_ready, 1)
            experts = [expert(t) for t in range(3)]
            for t in range(3):
                copy_w13(t, t, experts[t])
            copy_w2(0, 0, experts.pop(0))
            copy_aggT(G - 1)
            copy_xn2T(G - 2)
            add_x(G - 1)
            moments(G - 1, 1)
            dve.wait_ge(logits_mm, G - 1)
            nc.vector.tensor_copy(lg[:, 0, 0:TG], pLogits[:, 0:TG]).then_inc(logits_copied, 1)
            hidden(0, 0)
            for t in range(PEEL):
                tile_dve(t, t, experts)
            with dve.Fori(PEEL, TILES - RING, RING) as t:
                experts = [expert(t + 1), expert(t + 2)]
                for i in range(RING):
                    tile_dve(t + i, i, experts)
            experts = [expert(TILES - RING + 1), expert(TILES - RING + 2)]
            for i in range(RING):
                tile_dve(TILES - RING + i, i, experts)
                add_results(i)
            for n in range(RING, RING + LAST_PARTS):
                add_results(n)

        @block.tensor
        def _(pe):
            def aggregate(u, c):
                halves = known(u) and u >= U - 2
                if halves:
                    pe.wait_ge(last_half, u - (U - 2) + 1)
                else:
                    pe.wait_ge(e2_done, u + 1)
                for s in range(SRC):
                    k = SRC * c + s
                    if halves and s == HALF:
                        pe.wait_ge(e2_done, u + 1)
                    last = nc.tensor.matmul(pAgg[:], msg[:, k], w[:, c % 2, s], start=(k == 0), stop=(k == K - 1))
                last.then_inc(agg_done, 1)

            def back(g):
                pe.wait_ge(aggT_copied, g + 1)
                if not (known(g) and g == 0):
                    pe.wait_ge(x2_done, g)
                for b in range(TG):
                    last = nc.tensor.transpose(pX[:, b], aggT[:, b * P:(b + 1) * P], ident[:])
                last.then_inc(x2_T, 1)

            def transpose_xn2(g, h, bank=pXn):
                pe.wait_ge(xn2_ready, g + 1)
                if not (known(g) and g == 0):
                    pe.wait_ge(xn2T_copied, g)
                for b in range(TG):
                    last = nc.tensor.transpose(bank[:, b], rows[:, 0, TG * h + b, 0:D], ident[:])
                last.then_inc(xn2_T, 1)

            def logits(g, h, pr, bank=pLogits):
                pe.wait_ge(xn2T_copied, g + 1)
                if not (known(pr) and pr == 0):
                    pe.wait_ge(slots_ready, pr)
                for b in range(TG):
                    last = nc.tensor.matmul(bank[:, TG * h + b], xn2T[:, b * P:(b + 1) * P], rwT[:], start=True, stop=True)
                last.then_inc(logits_mm, 1)

            def rank(pr, pRank=pRank, pTot=pTot):
                pe.wait_ge(picked, 2 * pr + 2)
                nc.tensor.matmul(pRank, upper[:], chosen[:], start=True, stop=False, skip_group_check=True)
                for b in range(T2 - 1):
                    nc.tensor.matmul(pRank[:, b + 1:], ones[:], chosen[:, b:b + 1].to_broadcast([P, T2 - 1 - b, E]),
                                     start=False, stop=b == T2 - 2, skip_group_check=True)
                for b in range(T2):
                    last = nc.tensor.matmul(pTot, ones[:], chosen[:, b], start=b == 0, stop=b == T2 - 1,
                                            skip_group_check=True)
                last.then_inc(rank_mm, 1)

            def messages(n):
                if n >= 4:
                    pe.wait_ge(msg_ready, TG * (n - 3))
                for b in range(TG):
                    last = nc.tensor.matmul(pP[n % 4][:, b], xT[:, TG * n + b], wc[:], start=True, stop=True)
                last.then_inc(msg_mm, 1)

            def steps(pr, first=False):
                for j in range(PU):
                    u, c = PU * pr + j, j % C
                    if first and j == 1:
                        for n in range(4, K // TG):
                            messages(n)
                    if not first:
                        if j == 0:
                            back(2 * pr - 1)
                        if j == 1:
                            transpose_xn2(2 * pr - 2, 0)
                        if j == 2:
                            logits(2 * pr - 2, 0, pr - 1)
                        if j == 3:
                            transpose_xn2(2 * pr - 1, 1)
                        if j == 4:
                            logits(2 * pr - 1, 1, pr - 1)
                        if j == 5:
                            rank(pr - 1)
                    if j == 4:
                        back(2 * pr)
                    if first and j < C:
                        pe.wait_ge(msg_ready, SRC * (j + 1))
                    aggregate(u, c)

            pe.wait_ge(ops_ready, 1)
            pe.wait_ge(wg_loaded, 16)
            nc.tensor.matmul(pSm[:, 0:D], mean_op[:], wg[:], start=True, stop=True).then_inc(colmean_mm, 1)
            pe.wait_ge(ident_ready, 1)
            pe.wait_ge(x_loaded, 16)
            for n in range(K // TG):
                if n >= 4:
                    pe.wait_ge(xT_copied, n - 3)
                for b in range(TG):
                    last = nc.tensor.transpose(pP[n % 4][:, b], xs[:, TG * n + b], ident[:])
                last.then_inc(x_T, 1)
            pe.wait_ge(wc_ready, 1)
            pe.wait_ge(xT_copied, K // TG)
            for n in range(4):
                messages(n)
            steps(0, first=True)
            pe.wait_ge(rw_loaded, 16)
            pe.wait_ge(tables_ready, 1)
            with pe.Fori(1, PAIRS - 1) as pr:
                steps(pr)
            steps(PAIRS - 1)

            def turn(t, i):
                if known(t):
                    pe.wait_ge(xt_loaded[i % RING], 16 * (t // RING + 1))
                else:
                    pe.wait_ge(xt_loaded[i % RING], PER * (t - i % RING) + 16)
                if not (known(t) and t == 0):
                    pe.wait_ge(xtT_copied, t)
                nc.tensor.transpose(pXT, xt[:, i % RING, 0:D], ident[:]).then_inc(xt_T, 1)

            def up(t, i):
                if known(t) and t in (0, TILES - 1):
                    pe.wait_ge(xtT_copied, t + 1)
                pe.wait_ge(w13_copied, t + 1)
                if not (known(t) and t < 2):
                    pe.wait_ge(hid_ready, t - 1)
                for a in range(2):
                    for m in range(HT):
                        last = nc.tensor.matmul(pH[i % 2][0:HC, GW * a + P * m:GW * a + P * (m + 1)],
                                                w13[:, i % W_RING, a, HC * m:HC * (m + 1)], xtT[:, i % 2], start=True, stop=True)
                last.then_inc(h_mm, 1)

            def down(t, i):
                pe.wait_ge(hid_ready, t + 1)
                pe.wait_ge(w2_copied, t + 1)
                if not (known(t) and t == 0):
                    pe.wait_ge(y_out, t)
                for m in range(HT):
                    n = HC if m < HT - 1 else HL
                    last = nc.tensor.matmul(pY, hidT[0:n, i % 2, m * P:(m + 1) * P], w2e[0:n, i % 2, m * D:(m + 1) * D],
                                            start=m == 0, stop=m == HT - 1)
                last.then_inc(y_mm, 1)

            def tile_pe(t, i):
                if known(t):
                    if t == XN_AT:
                        pe.wait_ge(x2_done, G)
                        transpose_xn2(G - 1, 1, pX)
                    if t == LOGITS_AT:
                        logits(G - 1, 0, PAIRS - 1, pLogits_last)
                    if t == RANK_AT:
                        rank(PAIRS - 1, pRank_last, pTot_last)
                if not known(t) or t + 2 < TILES:
                    turn(t + 2, i + 2)
                if not known(t) or t + 1 < TILES:
                    up(t + 1, i + 1)
                if not known(t) or t > 0:
                    down(t - 1, i + 1)

            transpose_xn2(G - 2, 0)
            pe.wait_ge(aggT_copied, G)
            turn(0, 0)
            back(G - 1)
            logits(G - 2, 0, PAIRS - 1)
            turn(1, 1)
            pe.wait_ge(padding_zeroed, 1)
            up(0, 0)
            for t in range(PEEL):
                if t == 1:
                    pe.wait_ge(logits_copied, 1)
                tile_pe(t, t)
            with pe.Fori(PEEL, TILES - RING, RING) as t:
                for i in range(RING):
                    tile_pe(t + i, i)
            for t in range(TILES - RING, TILES):
                tile_pe(t, t)
            down(TILES - 1, RING - 1)



_INS = ['x', 'adj', 'L0_gnn_W', 'L0_gnn_B', 'L0_ffn_router_w', 'L0_ffn_w1', 'L0_ffn_w2', 'L0_ffn_w3']
_OUTS = [((4096, 128), 'float32')]


def kernel(**inputs):
    import numpy as _np
    import concourse.bacc as _bacc
    from concourse import mybir as _mybir
    from concourse.bass_utils import run_bass_kernel_spmd as _run

    laid = {name: _np.asarray(inputs[name]) for name in _INS}
    adj, w1, w2, w3 = laid['adj'], laid['L0_ffn_w1'], laid['L0_ffn_w2'], laid['L0_ffn_w3']
    n = adj.shape[0]
    e, h, d = w1.shape
    gw, c = TG * P, n // (SRC * P)
    laid['adj'] = adj.reshape(n // gw, gw, c, SRC, P).transpose(0, 2, 4, 3, 1).reshape(n // gw, c, P, SRC * gw)
    laid['L0_ffn_router_w'] = laid['L0_ffn_router_w'].T
    laid['L0_ffn_w1'], laid['L0_ffn_w3'] = w1.reshape(e * h, d).T, w3.reshape(e * h, d).T
    laid['L0_ffn_w2'] = w2.transpose(2, 0, 1)

    nc = _bacc.Bacc("TRN2", target_bir_lowering=False, num_devices=1)
    arrays, args = {}, []
    for name in _INS:
        a = _np.ascontiguousarray(laid[name])
        arrays[f"in_{name}_dram"] = a
        args.append(nc.dram_tensor(f"in_{name}_dram", a.shape, _mybir.dt.from_np(a.dtype), kind="ExternalInput").ap())
    for i, (shape, dtype) in enumerate(_OUTS):
        dt = _mybir.dt.from_np(_np.dtype(dtype))
        args.append(nc.dram_tensor(f"out_{i}_dram", shape, dt, kind="ExternalOutput").ap())
    gnn_moe_layer(nc, *args)
    r = _run(nc, [arrays], core_ids=[0])
    return r.results[0]["out_0_dram"]
```
